# Optimizing a Trainium2 kernel written in Bass

```python
import numpy as np
import jax
import jax.numpy as jnp

def _softmax(x, axis=-1):
    return jax.nn.softmax(x, axis=axis)

def _gelu(x):
    return jax.nn.gelu(x, approximate=True)

def _silu(x):
    return jax.nn.silu(x)

def _sigmoid(x):
    return jax.nn.sigmoid(x)

def _layernorm(x, axis=-1, eps=1e-05):
    m = jnp.mean(x, axis=axis, keepdims=True)
    v = jnp.var(x, axis=axis, keepdims=True)
    return (x - m) / jnp.sqrt(v + eps)

def _scatter_add(tgt, idx, src, axis=0):
    return tgt.at[idx].add(src)

def _segment_sum(src, seg, n):
    return jax.ops.segment_sum(src, seg, n)
kernel_name = 'mk_xattn_ffn_d1_seqx_r8_ae4e09'

def setup_inputs(seed: int=0):
    np.random.seed(seed)
    _w = jnp.asarray

    def _rec_inputs():
        import jax
        import jax.numpy as jnp
        _rk = jax.random.key(seed)
        x = 7.22e-05 + 1 * jax.random.normal(jax.random.fold_in(_rk, 1), (8, 128, 128), jnp.float32)
        _lenS = 128 - jax.random.randint(jax.random.fold_in(_rk, 7), (8,), 0, max(1, 128 // 4) + 1, jnp.int32)
        _lenS2 = 128 - jax.random.randint(jax.random.fold_in(_rk, 8), (8,), 0, max(1, 128 // 4) + 1, jnp.int32)
        _ctx_1024P = jax.random.normal(jax.random.fold_in(_rk, 11), (8, 16, 128), jnp.float32)
        _ctx_1024c = jax.random.dirichlet(jax.random.fold_in(_rk, 511), 0.3 * jnp.ones((16,), jnp.float32), (8, 128))
        _ctx_1024t = jnp.einsum('bsk,bkd->bsd', _ctx_1024c, _ctx_1024P)
        _ctx_1024t = _ctx_1024t * jax.lax.rsqrt(jnp.mean(jnp.square(_ctx_1024t)) + 1e-12) * 0.953939
        ctx_1024 = 4.13588e-05 + 0.999923 * (_ctx_1024t + 0.3 * jax.random.normal(jax.random.fold_in(_rk, 611), (8, 128, 128), jnp.float32))
        return (x, ctx_1024)
    x, ctx_1024 = _rec_inputs()

    def _L0_xattn_setup():
        import jax, jax.numpy as jnp
        import numpy as np
        N_HEAD = 16
        D_MODEL = 128
        D_K = D_MODEL // N_HEAD
        key = jax.random.key(seed)
        ks = jax.random.split(key, 11)
        B, S = (4, 256)
        s = 1.0 / np.sqrt(D_MODEL)
        return {'q': jax.random.normal(ks[0], (B, S, D_MODEL), jnp.float32), 'k': jax.random.normal(ks[1], (B, S, D_MODEL), jnp.float32), 'v': jax.random.normal(ks[2], (B, S, D_MODEL), jnp.float32), 'wq': jax.random.normal(ks[3], (D_MODEL, D_MODEL), jnp.float32) * s, 'bq': jax.random.normal(ks[4], (D_MODEL,), jnp.float32) * s, 'wk': jax.random.normal(ks[5], (D_MODEL, D_MODEL), jnp.float32) * s, 'bk': jax.random.normal(ks[6], (D_MODEL,), jnp.float32) * s, 'wv': jax.random.normal(ks[7], (D_MODEL, D_MODEL), jnp.float32) * s, 'bv': jax.random.normal(ks[8], (D_MODEL,), jnp.float32) * s, 'wo': jax.random.normal(ks[9], (D_MODEL, D_MODEL), jnp.float32) * s, 'bo': jax.random.normal(ks[10], (D_MODEL,), jnp.float32) * s}
    _L0_xattn_all = _L0_xattn_setup()
    _L0_xattn_in = {k: v for k, v in _L0_xattn_all.items() if k in ('wq', 'bq', 'wk', 'bk', 'wv', 'bv', 'wo', 'bo')}
    del _L0_xattn_all

    def _L0_ffn_setup():
        import jax, jax.numpy as jnp
        import numpy as np
        E = 32
        K = 4
        H = 128
        F = 128
        LIMIT = 7.0
        ALPHA = 1.702
        EPS = 1e-05

        def _rmsnorm(x, scale):
            t = x * jax.lax.rsqrt(jnp.mean(x * x, axis=-1, keepdims=True) + EPS)
            return t * scale

        def _swiglu(h):
            glu = jnp.minimum(h[..., ::2], LIMIT)
            lin = jnp.clip(h[..., 1::2], -LIMIT, LIMIT)
            return glu * jax.nn.sigmoid(ALPHA * glu) * (lin + 1.0)
        key = jax.random.key(seed)
        ks = jax.random.split(key, 8)
        B, S = (1, 128)
        x = jax.random.normal(ks[0], (B, S, H), dtype=jnp.float32)
        norm_scale = jnp.ones((H,), dtype=jnp.float32)
        gate_w = jax.random.normal(ks[1], (E, H), dtype=jnp.float32) * 0.02
        gate_b = jnp.zeros((E,), dtype=jnp.float32)
        w1 = jax.random.normal(ks[2], (E, 2 * F, H), dtype=jnp.float32) * 0.02
        b1 = jnp.zeros((E, 2 * F), dtype=jnp.float32)
        w2 = jax.random.normal(ks[3], (E, H, F), dtype=jnp.float32) * 0.02
        b2 = jnp.zeros((E, H), dtype=jnp.float32)
        return {'x': x, 'norm_scale': norm_scale, 'gate_w': gate_w, 'gate_b': gate_b, 'w1': w1, 'b1': b1, 'w2': w2, 'b2': b2}
    _L0_ffn_all = _L0_ffn_setup()
    _L0_ffn_in = {k: v for k, v in _L0_ffn_all.items() if k in ('norm_scale', 'gate_w', 'gate_b', 'w1', 'b1', 'w2', 'b2')}
    del _L0_ffn_all
    return {'x': x, 'ctx_1024': ctx_1024, 'L0_xattn_wq': _L0_xattn_in['wq'], 'L0_xattn_bq': _L0_xattn_in['bq'], 'L0_xattn_wk': _L0_xattn_in['wk'], 'L0_xattn_bk': _L0_xattn_in['bk'], 'L0_xattn_wv': _L0_xattn_in['wv'], 'L0_xattn_bv': _L0_xattn_in['bv'], 'L0_xattn_wo': _L0_xattn_in['wo'], 'L0_xattn_bo': _L0_xattn_in['bo'], 'L0_ffn_norm_scale': _L0_ffn_in['norm_scale'], 'L0_ffn_gate_w': _L0_ffn_in['gate_w'], 'L0_ffn_gate_b': _L0_ffn_in['gate_b'], 'L0_ffn_w1': _L0_ffn_in['w1'], 'L0_ffn_b1': _L0_ffn_in['b1'], 'L0_ffn_w2': _L0_ffn_in['w2'], 'L0_ffn_b2': _L0_ffn_in['b2']}

def reference(x, ctx_1024, L0_xattn_wq, L0_xattn_bq, L0_xattn_wk, L0_xattn_bk, L0_xattn_wv, L0_xattn_bv, L0_xattn_wo, L0_xattn_bo, L0_ffn_norm_scale, L0_ffn_gate_w, L0_ffn_gate_b, L0_ffn_w1, L0_ffn_b1, L0_ffn_w2, L0_ffn_b2):
    import jax
    import jax.numpy as jnp

    def _L0_xattn_ref(q, k, v, wq, bq, wk, bk, wv, bv, wo, bo):
        import jax, jax.numpy as jnp
        import numpy as np
        N_HEAD = 16
        D_MODEL = 128
        D_K = D_MODEL // N_HEAD
        B, S, _ = q.shape

        def proj(x, w, b):
            y = x @ w.T + b
            return y.reshape(B, -1, N_HEAD, D_K).transpose(0, 2, 1, 3)
        qh = proj(q, wq, bq)
        kh = proj(k, wk, bk)
        vh = proj(v, wv, bv)
        scale = jnp.sqrt(jnp.float32(D_K))
        scores = jnp.einsum('bhsd,bhtd->bhst', qh, kh) / scale
        attn = jax.nn.softmax(scores, axis=-1)
        out = jnp.einsum('bhst,bhtd->bhsd', attn, vh)
        out = out.transpose(0, 2, 1, 3).reshape(B, S, D_MODEL)
        return out @ wo.T + bo

    def _L0_ffn_ref(x, norm_scale, gate_w, gate_b, w1, b1, w2, b2):
        import jax, jax.numpy as jnp
        import numpy as np
        E = 32
        K = 4
        H = 128
        F = 128
        LIMIT = 7.0
        ALPHA = 1.702
        EPS = 1e-05

        def _rmsnorm(x, scale):
            t = x * jax.lax.rsqrt(jnp.mean(x * x, axis=-1, keepdims=True) + EPS)
            return t * scale

        def _swiglu(h):
            glu = jnp.minimum(h[..., ::2], LIMIT)
            lin = jnp.clip(h[..., 1::2], -LIMIT, LIMIT)
            return glu * jax.nn.sigmoid(ALPHA * glu) * (lin + 1.0)
        B, S, _ = x.shape
        t = _rmsnorm(x, norm_scale)
        g = t @ gate_w.T + gate_b
        tf = t.reshape(-1, H)
        gf = g.reshape(-1, E)
        T = tf.shape[0]
        vals, idx = jax.lax.top_k(gf, K)
        w = jax.nn.softmax(vals, axis=-1)
        combine = jnp.zeros((T, E), dtype=tf.dtype).at[jnp.arange(T)[:, None], idx].add(w)
        h1 = jnp.einsum('th,efh->tef', tf, w1) + b1
        h = _swiglu(h1)
        hw = h * combine[:, :, None]
        out = jnp.einsum('tef,ehf->th', hw, w2) + combine @ b2
        return x + out.reshape(B, S, H)
    x = x + _L0_xattn_ref(_layernorm(x, axis=-1), ctx_1024, ctx_1024, L0_xattn_wq, L0_xattn_bq, L0_xattn_wk, L0_xattn_bk, L0_xattn_wv, L0_xattn_bv, L0_xattn_wo, L0_xattn_bo)
    x = x + _L0_ffn_ref(_layernorm(x, axis=-1), L0_ffn_norm_scale, L0_ffn_gate_w, L0_ffn_gate_b, L0_ffn_w1, L0_ffn_b1, L0_ffn_w2, L0_ffn_b2)
    return x

_drawn_inputs = setup_inputs


def setup_inputs(seed=0):
    import zlib

    import numpy as np

    out = dict(_drawn_inputs(seed))
    spreads = {'L0_ffn_norm_scale': (1.0, 0.6),
     'L0_ffn_gate_b': (0.0, 0.46),
     'L0_ffn_b1': (0.0, 0.8),
     'L0_ffn_b2': (0.0, 0.336)}
    factors = {'L0_xattn_bq': 2.918, 'L0_xattn_bk': 8.0, 'L0_ffn_w1': 8.0, 'L0_ffn_w2': 7.645}
    for name, (base, spread) in spreads.items():
        noise = np.random.default_rng([zlib.crc32(name.encode()), seed]).standard_normal(out[name].shape)
        drawn = base * np.exp(spread * noise) if base else spread * noise
        out[name] = jnp.asarray(drawn.astype(out[name].dtype))
    for name, factor in factors.items():
        out[name] = (out[name] * factor).astype(out[name].dtype)
    return out
```

```python
from contextlib import ExitStack

import numpy as np

import concourse.bass as bass
from concourse import mybir

F32 = mybir.dt.float32
BF16 = mybir.dt.bfloat16
I32 = mybir.dt.int32
U32 = mybir.dt.uint32
ALU = mybir.AluOpType
ACT = mybir.ActivationFunctionType
AX = mybir.AxisListType

P = 128
B = 8
D = 128
H = 16
DK = D // H
G = 4
E = 32
K = 4
FF = 128
TOK = B * P
TILES = 64
PAIRS = TILES // 2
ROW = D + 4
LIMIT = 7.0
ALPHA = 1.702
EPS = 1e-5

C_ID, C_TRI, C_IOTA, C_BASE, C_CODE, C_P, C_DUMMY, C_STEP = 0, 128, 256, 288, 320, 352, 353, 417
C_END = C_STEP + B


def shape_constants():
    c = np.zeros((P, C_END), np.float32)
    p = np.arange(P)
    c[:, C_ID:C_ID + P] = np.eye(P)
    c[:, C_TRI:C_TRI + P] = p[:, None] < p[None, :]
    c[:, C_IOTA:C_IOTA + E] = np.arange(E)
    c[:, C_BASE:C_BASE + E] = TOK * np.arange(E)
    b, k = np.meshgrid(np.arange(B), np.arange(K), indexing="ij")
    c[:, C_CODE:C_CODE + B * K] = (k * TOK + b * P).reshape(-1)[None, :] + p[:, None]
    c[:, C_P] = p
    c[:, C_DUMMY:C_DUMMY + TILES] = K * TOK + P * np.arange(TILES)[None, :] + p[:, None]
    c[:, C_STEP:C_STEP + B] = P * np.arange(B)
    return c


def build(nc, x, ctxT, wq, bq, wk, bk, wvT, bv, woT, bo, scale, gateT, gate_b, w1T, w2T, b12, consts, out):
    ctx = ExitStack()

    def sb(name, shape, dt=F32):
        return ctx.enter_context(nc.sbuf_tensor(name, shape, dt))

    def sem(name):
        return ctx.enter_context(nc.semaphore(name))

    with ctx:
        routed = nc.dram_tensor("routed", (E * TOK, ROW), F32, kind="Internal").ap()
        returned = nc.dram_tensor("returned", (K * TOK + TILES * P, D), F32, kind="Internal").ap()
        bias_d = nc.dram_tensor("bias_parts", (3, P * 96), BF16, kind="Internal").ap()

        x_sb = sb("x_sb", [P, B, D])
        xbo = sb("xbo", [P, B, D])
        cT = sb("cT", [P, 2, P])
        wq_sb = sb("wq_sb", [P, G, P])
        wk_sb = sb("wk_sb", [P, G, P])
        bqk = sb("bqk", [P, 2, G])
        wv_sb = sb("wv_sb", [P, D])
        wo_sb = sb("wo_sb", [P, D])
        bv_sb = sb("bv_sb", [P, D])
        bo_sb = sb("bo_sb", [P, D])
        sc_sb = sb("sc_sb", [P, D])
        gate_sb = sb("gate_sb", [P, E])
        gb_sb = sb("gb_sb", [P, E])
        cst = sb("cst", [P, C_END])
        w1_sb = sb("w1_sb", [P, E, 2 * FF])
        w2_sb = sb("w2_sb", [P, E, D])
        b_sb = sb("b_sb", [P, 96])
        b_res = sb("b_res", [P, 2, 96])
        b_part = sb("b_part", [P, 3, 96], BF16)
        bias_rows = sb("bias_rows", [3, P * 96], BF16)
        tri_bf = sb("tri_bf", [P, P], BF16)
        ones_bf = sb("ones_bf", [P, P], BF16)
        ones_f = sb("ones_f", [P, P])
        zeros = sb("zeros", [P, ROW])
        ident = cst[:, C_ID:C_ID + P]
        st1 = sb("st1", [P, B, 6])
        mv1 = sb("mv1", [P, B, 2])
        ve1 = sb("ve1", [P, B])
        rs1 = sb("rs1", [P, B])
        half_neg = sb("half_neg", [P, B])
        y = sb("y", [P, D])
        yT = sb("yT", [P, P])
        qT = sb("qT", [P, G, P])
        kT = sb("kT", [P, G, P])
        v_ext = sb("v_ext", [P, 2, H, 32])
        prob = sb("prob", [P, G, G, P])
        mx = sb("mx", [P, 2, 8])
        pT = sb("pT", [P, G, G, P])
        oT = sb("oT", [P, G, P])
        rden = sb("rden", [P, G, G, 1])
        on = sb("on", [P, D])
        onT = sb("onT", [P, P])
        x2 = sb("x2", [P, B, D])
        st2 = sb("st2", [P, 6])
        mv2 = sb("mv2", [P, 2])
        ve2 = sb("ve2", [P, 2])
        rs2 = sb("rs2", [P, 2])
        z = sb("z", [P, D])
        xr = sb("xr", [P, B, D])
        tmp = sb("tmp", [P, D])
        rows = sb("rows", [P, 2, K, ROW])
        tT = sb("tT", [P, P])
        g_sb = sb("g_sb", [P, E])
        top = sb("top", [P, 8])
        topi = sb("topi", [P, 8], U32)
        ntop = sb("ntop", [P, 1])
        ew = sb("ew", [P, K])
        sw = sb("sw", [P, 1])
        rsw = sb("rsw", [P, 1])
        w_all = sb("w_all", [P, B, K])
        hot = sb("hot", [P, K, E])
        m_bf = sb("m_bf", [P, E], BF16)
        m_sum = sb("m_sum", [P, E], BF16)
        place = sb("place", [P, E])
        pl_hot = sb("pl_hot", [P, K, E])
        pos = sb("pos", [P, 2, K], U32)
        cnt = sb("cnt", [TILES, E])
        over = sb("over", [TILES, E, B])
        nt = sb("nt", [TILES, E])
        ones_e = sb("ones_e", [TILES, E])
        incl = sb("incl", [TILES, E])
        excl = sb("excl", [TILES, E])
        past = sb("past", [TILES, E])
        plan = sb("plan", [TILES, 4])
        ecol = sb("ecol", [TILES, 1])
        e_hot = sb("e_hot", [TILES, E])
        junk = sb("junk", [TILES, 2, E])
        base_i = sb("base_i", [TILES, 1])
        cnt_i = sb("cnt_i", [TILES, 1])
        a_i = sb("a_i", [TILES, 1])
        m_i = sb("m_i", [TILES, 1])
        r0_i = sb("r0_i", [TILES, 1])
        diag = sb("diag", [TILES, 4, TILES])
        tab = sb("tab", [1, 2, TILES], I32)
        inv = sb("inv", [P, 3, TILES])
        aside = sb("aside", [P, TILES])
        xt = sb("xt", [P, 2, 2, ROW])
        xtT = sb("xtT", [P, 2, 2, P])
        glu = sb("glu", [P, 2, 2, FF])
        lin = sb("lin", [P, 2, 2, FF])
        sg = sb("sg", [P, 2, 2, FF])
        gs = sb("gs", [P, 2, 2, FF])
        hid = sb("hid", [P, 2, 2, FF])
        hidT = sb("hidT", [P, 2, 2, P])
        y_sb = sb("y_sb", [P, 2, 2, D])
        dest = sb("dest", [P, 2, 2], U32)
        dest_all = sb("dest_all", [P, TILES], U32)
        fin = sb("fin", [P, B, K, D])
        acc = sb("acc", [P, B, D])

        bank = [ctx.enter_context(nc.psum_tensor(f"bank{i}", [P, 512], F32)) for i in range(8)]

        def scores_of(half):
            return [bank[2 * half], bank[2 * half + 1]]

        x_ld = sem("x_ld")
        w_ld = sem("w_ld")
        ln_ld = sem("ln_ld")
        c_ld = [sem("c_ld0"), sem("c_ld1")]
        ffw_ld = sem("ffw_ld")
        bias_ld = sem("bias_ld")
        zero_set = sem("zero_set")
        filled = sem("filled")
        const_set = sem("const_set")
        pool_set = sem("pool_set")
        st1_done = sem("st1_done")
        mv1_done = sem("mv1_done")
        pool_turn = sem("pool_turn")
        dve_turn = sem("dve_turn")
        ve1_done = sem("ve1_done")
        rs1_done = sem("rs1_done")
        xbo_done = sem("xbo_done")
        bsplit = sem("bsplit")
        bias_out = sem("bias_out")
        y_done = sem("y_done")
        yT_mm = sem("yT_mm")
        yT_done = sem("yT_done")
        k_mm = sem("k_mm")
        k_done = sem("k_done")
        q_mm = sem("q_mm")
        q_done = sem("q_done")
        v_mm = sem("v_mm")
        v_done = sem("v_done")
        s_mm = [sem("sA_mm"), sem("sB_mm")]
        max_done = [sem("maxA"), sem("maxB")]
        sub_done = [sem("subA"), sem("subB")]
        exp_done = [sem("expA"), sem("expB")]
        pT_mm = sem("pT_mm")
        pT_done = sem("pT_done")
        pv_mm = sem("pv_mm")
        oT_done = sem("oT_done")
        o_mm = sem("o_mm")
        rden_done = sem("rden_done")
        on_done = sem("on_done")
        onT_mm = sem("onT_mm")
        onT_done = sem("onT_done")
        wo_mm = sem("wo_mm")
        x2_done = sem("x2_done")
        z_done = sem("z_done")
        xr_done = sem("xr_done")
        st2_done = sem("st2_done")
        mv2_done = sem("mv2_done")
        ve2_done = sem("ve2_done")
        rs2_done = sem("rs2_done")
        tmp_done = sem("tmp_done")
        t_done = sem("t_done")
        rows_done = sem("rows_done")
        tT_mm = sem("tT_mm")
        tT_done = sem("tT_done")
        gate_mm = sem("gate_mm")
        g_done = sem("g_done")
        top_done = sem("top_done")
        topi_done = sem("topi_done")
        ntop_done = sem("ntop_done")
        ew_done = sem("ew_done")
        rsw_done = sem("rsw_done")
        w_done = sem("w_done")
        hot_done = sem("hot_done")
        m_done = sem("m_done")
        rank_mm = sem("rank_mm")
        msum_done = sem("msum_done")
        place_done = sem("place_done")
        plhot_done = sem("plhot_done")
        pos_done = sem("pos_done")
        sent = [sem("sent0"), sem("sent1")]
        cnt_mm = sem("cnt_mm")
        plan_step = sem("plan_step")
        diag_done = sem("diag_done")
        plan_mm = sem("plan_mm")
        tab_done = sem("tab_done")
        inv_done = sem("inv_done")
        aside_done = sem("aside_done")
        xt_ld = [sem("xt_ld0"), sem("xt_ld1")]
        xtT_mm = sem("xtT_mm")
        xtT_done = sem("xtT_done")
        h_mm = sem("h_mm")
        glu_done = sem("glu_done")
        lin_done = sem("lin_done")
        sg_done = sem("sg_done")
        gs_done = sem("gs_done")
        hid_done = sem("hid_done")
        hidT_mm = sem("hidT_mm")
        hidT_done = sem("hidT_done")
        y_mm = sem("y_mm")
        ysb_done = sem("ysb_done")
        dest_done = sem("dest_done")
        code_done = sem("code_done")
        back = [sem("back0"), sem("back1")]
        fin_ld = [sem(f"fin_ld{b}") for b in range(B)]
        acc_done = sem("acc_done")
        out_st = sem("out_st")

        bqk_ld = 16

        block = ctx.enter_context(nc.Block())

        def first(n):
            return isinstance(n, int) and n == 0

        def steps(fn, engine):
            fn(0, 0, True, False, False)
            fn(0, 1, True, True, False)
            with engine.Fori(1, B // 2) as n:
                fn(n, 0, True, True, True)
                fn(n, 1, True, True, True)
            fn(B // 2, 0, False, True, True)
            fn(B // 2, 1, False, False, True)

        def pair_steps(fn, engine):
            fn(0, 0, True, True, False, False)
            fn(0, 1, True, True, True, False)
            with engine.Fori(1, PAIRS // 2 - 1) as n:
                fn(n, 0, True, True, True, True)
                fn(n, 1, True, True, True, True)
            fn(PAIRS // 2 - 1, 0, True, True, True, True)
            fn(PAIRS // 2 - 1, 1, False, True, True, True)
            fn(PAIRS // 2, 0, False, False, True, True)
            fn(PAIRS // 2, 1, False, False, False, True)

        @block.sync
        def _(sp):
            sp.dma_start(x_sb[:, :, :], x.rearrange("(b p) d -> p b d", p=P)).then_inc(x_ld, 16)
            sp.dma_start(cst[:, :], consts).then_inc(w_ld, 16)
            sp.dma_start(cT[:, 0, :], ctxT[:, 0:P]).then_inc(c_ld[0], 16)
            sp.dma_start(wk_sb[:, :, :], wk).then_inc(w_ld, 16)
            sp.dma_start(wq_sb[:, :, :], wq).then_inc(w_ld, 16)
            sp.dma_start(bqk[:, 0, :], bq).then_inc(w_ld, 16)
            sp.dma_start(bqk[:, 1, :], bk).then_inc(w_ld, 16)
            sp.dma_start(wv_sb[:, :], wvT).then_inc(w_ld, 16)
            sp.dma_start(cT[:, 1, :], ctxT[:, P:2 * P]).then_inc(c_ld[1], 16)
            sp.dma_start(wo_sb[:, :], woT).then_inc(w_ld, 16)
            sp.dma_start(gate_sb[:, :], gateT).then_inc(w_ld, 16)
            sp.dma_start(b_sb[:, :], b12).then_inc(bias_ld, 16)
            for b in range(B):
                if b >= 2:
                    sp.wait_ge(v_mm, b - 1)
                    sp.dma_start(cT[:, b % 2, :], ctxT[:, b * P:(b + 1) * P]).then_inc(c_ld[b % 2], 16)
                e0, e1 = b * E // B, (b + 1) * E // B
                sp.dma_start(w1_sb[:, e0:e1, :], w1T[:, e0:e1, :]).then_inc(ffw_ld, 16)
                sp.dma_start(w2_sb[:, e0:e1, :], w2T[:, e0:e1, :]).then_inc(ffw_ld, 16)

            sp.wait_ge(tab_done, 1)
            for par in range(2):
                sp.wait_ge(sent[par], 16 * K * (B // 2))

            def load_pair(n, par, again):
                for h in range(2):
                    r = sp.value_load(tab[0:1, 1, bass.ds(4 * n + 2 * par + h, 1)], min_val=0, max_val=E * TOK - P)
                    if again and h == 0:
                        sp.wait_ge(xtT_mm, 2 * n + par - 1)
                        sp.wait_ge(code_done, 2 * n + par - 1)
                    sp.dma_start(xt[:, par, h, :], routed[bass.ds(r, P), :]).then_inc(xt_ld[par], 16)

            load_pair(0, 0, False)
            load_pair(0, 1, False)
            with sp.Fori(1, PAIRS // 2) as n:
                load_pair(n, 0, True)
                load_pair(n, 1, True)

            for par in range(2):
                sp.wait_ge(back[par], 16 * PAIRS)
            for b in range(B):
                src = returned[0:K * TOK, :].rearrange("(k b p) d -> b p k d", k=K, p=P)
                sp.dma_start(fin[:, b, :, :], src[b]).then_inc(fin_ld[b], 16)
            for b in range(B):
                sp.wait_ge(acc_done, K * (b + 1))
                sp.dma_start(out[b * P:(b + 1) * P, :], acc[:, b, :]).then_inc(out_st, 16)
            sp.wait_ge(out_st, 16 * B)

        @block.gpsimd
        def _(pool):
            pool.memset(zeros[:, :], 0.0).then_inc(zero_set, 1)
            pool.memset(half_neg[:, :], -0.5).then_inc(pool_set, 1)
            pool.memset(v_ext[:, :, :, :], 0.0).then_inc(pool_set, 1)
            pool.memset(m_sum[:, :], 0.0).then_inc(pool_set, 1)
            pool.memset(rows[:, :, :, :], 0.0).then_inc(pool_set, 1)
            pool.wait_ge(pool_set, 2)
            pool.memset(v_ext[:, :, :, DK:DK + 1], 1.0).then_inc(pool_set, 1)
            pool.wait_ge(ve1_done, 1)
            pool.tensor_tensor(rs1[:, :], ve1[:, :], half_neg[:, :], ALU.pow).then_inc(rs1_done, 1)
            pool.wait_ge(x_ld, 16)
            pool.wait_ge(ln_ld, 64)
            pool.tensor_tensor(xbo[:, :, :], x_sb[:, :, :], bo_sb[:, None, :].to_broadcast([P, B, D]),
                               ALU.add).then_inc(xbo_done, 1)

            def step(n, par, a, f, c):
                t = 2 * n + par
                rn, rp = (n - 1, par)
                if c:
                    pool.wait_ge(rank_mm, t - 1)
                    pool.wait_ge(m_done, t - 1)
                    pool.tensor_tensor(m_sum[:, :], m_sum[:, :], m_bf[:, :], ALU.add).then_inc(msum_done, 1)
                    pool.wait_ge(pos_done, t - 1)
                    pool.wait_ge(rows_done, t - 1)
                    pool.wait_ge(filled, 16)
                    pool.sem_inc(pool_turn, 1)
                    for k in range(K):
                        pool.indirect_dma_start(
                            out=routed, out_offset=bass.IndirectOffsetOnAxis(ap=pos[:, par, k:k + 1], axis=0),
                            in_=rows[:, par, k, :], in_offset=None).then_inc(sent[par], 16)
                if f:
                    fp = 1 - par
                    pool.wait_ge(ve2_done, t)
                    pool.tensor_tensor(rs2[:, :], ve2[:, :], half_neg[:, 0:2], ALU.pow).then_inc(rs2_done, 1)
                    pool.wait_ge(z_done, t)
                    pool.tensor_tensor(xr[:, bass.ds(t - 1, 1), :], z[:, :], x2[:, bass.ds(t - 1, 1), :],
                                       ALU.add).then_inc(xr_done, 1)
                    pool.wait_ge(t_done, t)
                    if not first(n):
                        pool.wait_ge(sent[fp], 16 * K * (n if par == 1 else n - 1))
                    pool.wait_ge(pool_set, 5)
                    pool.sem_inc(pool_turn, 1)
                    pool.tensor_copy(rows[:, fp, 1:K, 0:D], rows[:, fp, 0:1, 0:D].to_broadcast([P, K - 1, D]))
                    code = cst[:, bass.ds(C_CODE + K * (t - 1), K)]
                    pool.tensor_copy(rows[:, fp, :, D], code).then_inc(rows_done, 1)

            steps(step, pool)

            def pstep(n, par, xin, work, mid, end):
                if end:
                    q = 2 * n + par - 2
                    pool.wait_ge(ysb_done, q + 1)
                    pool.wait_ge(dest_done, q + 1)
                    pool.sem_inc(pool_turn, 1)
                    for h in range(2):
                        pool.indirect_dma_start(
                            out=returned,
                            out_offset=bass.IndirectOffsetOnAxis(ap=dest[:, par, h:h + 1], axis=0),
                            in_=y_sb[:, par, h, :], in_offset=None).then_inc(back[par], 16)

            pair_steps(pstep, pool)

        @block.scalar
        def _(act):
            act.wait_ge(zero_set, 1)
            act.dma_start(routed.rearrange("(e r) c -> r e c", e=E)[0:P],
                          zeros[:, None, :].to_broadcast([P, E, ROW])).then_inc(filled, 16)
            act.dma_start(bo_sb[:, :], bo.to_broadcast([P, D])).then_inc(ln_ld, 16)
            act.dma_start(bv_sb[:, :], bv.to_broadcast([P, D])).then_inc(ln_ld, 16)
            act.dma_start(sc_sb[:, :], scale.to_broadcast([P, D])).then_inc(ln_ld, 16)
            act.dma_start(gb_sb[:, :], gate_b.to_broadcast([P, E])).then_inc(ln_ld, 16)
            act.wait_ge(bsplit, 5)
            act.dma_start(bias_d[:, 0:P * 64].rearrange("r (p c) -> p r c", p=P), b_part[:, :, 0:64]).then_inc(bias_out, 16)
            act.dma_start(bias_d[:, P * 64:].rearrange("r (p c) -> p r c", p=P), b_part[:, :, 64:96]).then_inc(bias_out, 16)
            act.wait_ge(bias_out, 32)
            act.dma_start(bias_rows[:, :], bias_d).then_inc(bias_out, 16)

            def copy(dst, src):
                return act.activation(dst, src, ACT.Copy)

            def exp_half(half):
                sl = prob[:, 2 * half:2 * half + 2, :, :]
                return act.activation(sl, sl, ACT.Exp, scale=float(DK) ** -0.5)

            def step(n, par, a, f, c):
                t = 2 * n + par
                if c:
                    act.wait_ge(tT_mm, t - 1)
                    copy(tT[:, :], bank[6][:, 0:P]).then_inc(tT_done, 1)
                if a:
                    act.wait_ge(k_mm, t + 1)
                    for g in range(G):
                        ins = act.activation(kT[:, g, :], bank[7][:, g * P:(g + 1) * P], ACT.Identity,
                                             bias=bqk[:, 1, g:g + 1])
                    ins.then_inc(k_done, 1)
                if f:
                    act.wait_ge(sub_done[1], t)
                    exp_half(1).then_inc(exp_done[1], 1)
                    act.wait_ge(pT_mm, 4 * (t - 1) + 1)
                    copy(pT[:, 0, :, :], bank[4][:, :]).then_inc(pT_done, 1)
                if a:
                    act.wait_ge(yT_mm, t + 1)
                    copy(yT[:, :], bank[7][:, 0:P]).then_inc(yT_done, 1)
                if f:
                    act.wait_ge(pT_mm, 4 * (t - 1) + 2)
                    copy(pT[:, 1, :, :], bank[5][:, :]).then_inc(pT_done, 1)
                if a:
                    act.wait_ge(q_mm, t + 1)
                    for g in range(G):
                        ins = act.activation(qT[:, g, :], bank[6][:, g * P:(g + 1) * P], ACT.Identity,
                                             bias=bqk[:, 0, g:g + 1])
                    ins.then_inc(q_done, 1)
                if f:
                    for j in (2, 3):
                        act.wait_ge(pT_mm, 4 * (t - 1) + j + 1)
                        copy(pT[:, j, :, :], bank[2 + j][:, :]).then_inc(pT_done, 1)
                if c:
                    act.wait_ge(ntop_done, t - 1)
                    act.activation(ew[:, :], top[:, 0:K], ACT.Exp, bias=ntop[:, 0:1],
                                   accum_out=sw[:, 0:1]).then_inc(ew_done, 1)
                if f:
                    act.wait_ge(pv_mm, t)
                    copy(oT[:, :, :], bank[7][:, :]).then_inc(oT_done, 1)
                    act.wait_ge(onT_mm, t)
                    copy(onT[:, :], bank[7][:, 0:P]).then_inc(onT_done, 1)
                if a:
                    act.wait_ge(sub_done[0], t + 1)
                    exp_half(0).then_inc(exp_done[0], 1)

            steps(step, act)

            def pstep(n, par, xin, work, mid, end):
                q = 2 * n + par
                if xin:
                    act.wait_ge(xtT_mm, q + 2)
                    copy(xtT[:, 1 - par, :, :], bank[5 - par][:, 0:2 * P]).then_inc(xtT_done, 1)
                if work:
                    act.wait_ge(glu_done, q + 1)
                    act.activation(sg[:, par, :, :], glu[:, par, :, :], ACT.Sigmoid, scale=ALPHA).then_inc(sg_done, 1)
                if end:
                    act.wait_ge(y_mm, q - 1)
                    if not (isinstance(n, int) and n < 2):
                        act.wait_ge(back[par], 32 * (n - 1))
                    copy(y_sb[:, par, :, :], bank[2 + par][:, 0:2 * D]).then_inc(ysb_done, 1)
                if mid:
                    act.wait_ge(hidT_mm, q)
                    copy(hidT[:, 1 - par, :, :], bank[7 - par][:, 0:2 * P]).then_inc(hidT_done, 1)

            act.wait_ge(xtT_mm, 1)
            copy(xtT[:, 0, :, :], bank[4][:, 0:2 * P]).then_inc(xtT_done, 1)
            pair_steps(pstep, act)

        @block.tensor
        def _(pe):
            pe.wait_ge(w_ld, 16 * 8)
            pe.wait_ge(const_set, 3)

            def score_heads(half, groups):
                for g in groups:
                    for jj in range(2):
                        j = 2 * half + jj
                        ins = pe.matmul(scores_of(half)[jj][:, g * P:(g + 1) * P],
                                        qT[32 * j:32 * j + DK, g, :], kT[32 * j:32 * j + DK, g, :],
                                        start=True, stop=True)
                return ins

            def turn_probs(t, j):
                if j >= 2 or not isinstance(t, int) or t >= 2:
                    pe.wait_ge(pT_done, 4 * (t - 1) + j - 1)
                for g in range(G):
                    ins = pe.transpose(bank[4 + j % 2][:, g * P:(g + 1) * P], prob[:, j, g, :], ident)
                ins.then_inc(pT_mm, 1)

            def step(n, par, a, f, c):
                t = 2 * n + par
                if c:
                    pe.wait_ge(t_done, t - 1)
                    pe.transpose(bank[6][:, 0:P], rows[:, par, 0, 0:D], ident).then_inc(tT_mm, 1)
                if a:
                    pe.wait_ge(c_ld[par], 16 * n + 16)
                    if f and c:
                        pe.wait_ge(onT_done, t - 1)
                    if f and not c:
                        pe.wait_ge(yT_done, t)
                    for g in range(G):
                        ins = pe.matmul(bank[7][:, g * P:(g + 1) * P], wk_sb[:, g, :], cT[:, par, :],
                                        start=True, stop=True)
                    ins.then_inc(k_mm, 1)
                if c:
                    pe.wait_ge(tT_done, t - 1)
                    pe.matmul(bank[6][:, 0:E], tT[:, :], gate_sb[:, :], start=True, stop=True).then_inc(gate_mm, 1)
                if f:
                    pe.wait_ge(exp_done[0], t)
                    turn_probs(t, 0)
                if a:
                    pe.wait_ge(y_done, t + 1)
                    pe.wait_ge(k_done, t + 1)
                    pe.transpose(bank[7][:, 0:P], y[:, :], ident).then_inc(yT_mm, 1)
                if f:
                    turn_probs(t, 1)
                if a:
                    pe.wait_ge(yT_done, t + 1)
                    if c:
                        pe.wait_ge(g_done, t - 1)
                    elif f:
                        pe.wait_ge(v_done, t)
                    for g in range(G):
                        ins = pe.matmul(bank[6][:, g * P:(g + 1) * P], wq_sb[:, g, :], yT[:, :],
                                        start=True, stop=True)
                    ins.then_inc(q_mm, 1)
                if c:
                    pe.wait_ge(m_done, t - 1)
                    if not (isinstance(n, int) and n == 1 and par == 0):
                        pe.wait_ge(msum_done, t - 2)
                    pe.matmul(bank[7][:, 0:E], tri_bf[:, :], m_bf[:, :], start=True, stop=False)
                    pe.matmul(bank[7][:, 0:E], ones_bf[:, :], m_sum[:, :], start=False, stop=True).then_inc(rank_mm, 1)
                if f:
                    pe.wait_ge(exp_done[1], t)
                    turn_probs(t, 2)
                if a:
                    pe.wait_ge(q_done, t + 1)
                    pe.matmul(bank[6][:, 0:D], cT[:, par, :], wv_sb[:, :], start=True, stop=True).then_inc(v_mm, 1)
                if f:
                    turn_probs(t, 3)
                if a:
                    if f:
                        pe.wait_ge(sub_done[0], t)
                    score_heads(0, range(G)).then_inc(s_mm[0], 1)
                if f:
                    pe.wait_ge(pT_done, 4 * t)
                    if c:
                        pe.wait_ge(place_done, t - 1)
                    for g in range(G):
                        for j in range(G):
                            ins = pe.matmul(bank[7][32 * j:32 * j + 32, g * P:(g + 1) * P],
                                            v_ext[:, 1 - par, 4 * g + j, :], pT[:, j, g, :],
                                            start=True, stop=True)
                    ins.then_inc(pv_mm, 1)
                if a:
                    if f:
                        pe.wait_ge(sub_done[1], t)
                    score_heads(1, range(0, 2))
                if f:
                    pe.wait_ge(oT_done, t)
                    if a:
                        pe.wait_ge(v_done, t + 1)
                    elif c:
                        pe.wait_ge(g_done, t - 1)
                    for g in range(G):
                        ins = pe.transpose(bank[6][:, g * P:(g + 1) * P], oT[:, g, :], ident)
                    ins.then_inc(o_mm, 1)
                if a:
                    score_heads(1, range(2, 4)).then_inc(s_mm[1], 1)
                if f:
                    pe.wait_ge(on_done, t)
                    pe.transpose(bank[7][:, 0:P], on[:, :], ident).then_inc(onT_mm, 1)
                    pe.wait_ge(onT_done, t)
                    pe.matmul(bank[6][:, 0:D], onT[:, :], wo_sb[:, :], start=True, stop=True).then_inc(wo_mm, 1)

            steps(step, pe)

            pe.wait_ge(msum_done, B)
            pe.wait_ge(place_done, B)
            pe.matmul(bank[7][0:TILES, 0:E], ones_bf[:, 0:TILES], m_sum[:, :], start=True, stop=True).then_inc(cnt_mm, 1)
            pe.wait_ge(diag_done, 1)
            pe.matmul(bank[6][:, 0:4 * TILES], ones_f[0:TILES, :], diag[:, :, :], start=True, stop=True).then_inc(plan_mm, 1)

            def turn_rows(n, par):
                pe.wait_ge(xt_ld[par], 32 * n + 32)
                for h in range(2):
                    ins = pe.transpose(bank[4 + par][:, h * P:(h + 1) * P], xt[:, par, h, 0:D], ident)
                ins.then_inc(xtT_mm, 1)

            def pstep(n, par, xin, work, mid, end):
                q = 2 * n + par
                if xin:
                    pe.wait_ge(xtT_done, q)
                    turn_rows(n if par == 0 else n + 1, 1 - par)
                if work:
                    ex = [pe.value_load(tab[0:1, 0, bass.ds(4 * n + 2 * par + h, 1)], min_val=0, max_val=E - 1)
                          for h in range(2)]
                    pe.wait_ge(xtT_done, q + 1)
                    if not (isinstance(n, int) and n == 0):
                        pe.wait_ge(lin_done, q - 1)
                    for h in range(2):
                        dst = bank[par][:, h * 2 * FF:(h + 1) * 2 * FF]
                        pe.matmul(dst, ones_bf[0:3, :], bias_rows[0:3, bass.ds(ex[h] * (2 * FF), 2 * FF)],
                                  start=True, stop=False)
                        ins = pe.matmul(dst, xtT[:, par, h, :], w1_sb[:, bass.ds(ex[h], 1), :],
                                        start=False, stop=True)
                    ins.then_inc(h_mm, 1)
                if end:
                    ex = [pe.value_load(tab[0:1, 0, bass.ds(4 * n + 2 * par + h - 4, 1)], min_val=0, max_val=E - 1)
                          for h in range(2)]
                    pe.wait_ge(hidT_done, q - 1)
                    for h in range(2):
                        dst = bank[2 + par][:, h * D:(h + 1) * D]
                        pe.matmul(dst, ones_bf[0:3, :], bias_rows[0:3, bass.ds(ex[h] * D + E * 2 * FF, D)],
                                  start=True, stop=False)
                        ins = pe.matmul(dst, hidT[:, par, h, :], w2_sb[:, bass.ds(ex[h], 1), :],
                                        start=False, stop=True)
                    ins.then_inc(y_mm, 1)
                if mid:
                    pe.wait_ge(hid_done, q)
                    if not (isinstance(n, int) and (n == 0 or (n == 1 and par == 0))):
                        pe.wait_ge(hidT_done, q - 2)
                    for h in range(2):
                        ins = pe.transpose(bank[7 - par][:, h * P:(h + 1) * P], hid[:, 1 - par, h, :], ident)
                    ins.then_inc(hidT_mm, 1)

            pe.wait_ge(ffw_ld, 16 * 2 * B)
            pe.wait_ge(bias_out, 48)
            pe.wait_ge(inv_done, 1)
            turn_rows(0, 0)
            pair_steps(pstep, pe)

        @block.vector
        def _(dve):
            dve.wait_ge(x_ld, 16)
            for b in range(B):
                dve.bn_stats(st1[:, b, :], x_sb[:, b, :]).then_inc(st1_done, 1)
            for b in range(B):
                dve.wait_ge(st1_done, b + 1)
                dve.bn_aggr(mv1[:, b, :], st1[:, b, :]).then_inc(mv1_done, 1)
            dve.wait_ge(mv1_done, B)
            dve.tensor_scalar(ve1[:, :], mv1[:, :, 1], EPS, None, ALU.add).then_inc(ve1_done, 1)
            dve.wait_ge(w_ld, 16 * 8)
            dve.tensor_copy(tri_bf[:, :], cst[:, C_TRI:C_TRI + P]).then_inc(const_set, 1)
            dve.memset(ones_bf[:, :], 1.0).then_inc(const_set, 1)
            dve.memset(ones_f[:, :], 1.0).then_inc(const_set, 1)
            dve.memset(ones_e[:, :], 1.0).then_inc(const_set, 1)
            dve.wait_ge(bias_ld, 16)
            dve.tensor_copy(b_part[:, 0, :], b_sb[:, :]).then_inc(bsplit, 1)
            dve.wait_ge(bsplit, 1)
            dve.tensor_tensor(b_res[:, 0, :], b_sb[:, :], b_part[:, 0, :], ALU.subtract).then_inc(bsplit, 1)
            dve.wait_ge(bsplit, 2)
            dve.tensor_copy(b_part[:, 1, :], b_res[:, 0, :]).then_inc(bsplit, 1)
            dve.wait_ge(bsplit, 3)
            dve.tensor_tensor(b_res[:, 1, :], b_res[:, 0, :], b_part[:, 1, :], ALU.subtract).then_inc(bsplit, 1)
            dve.wait_ge(bsplit, 4)
            dve.tensor_copy(b_part[:, 2, :], b_res[:, 1, :]).then_inc(bsplit, 1)
            dve.wait_ge(rs1_done, 1)
            dve.wait_ge(pool_set, 5)
            dve.wait_ge(xbo_done, 1)

            def heads(half):
                return prob[:, 2 * half:2 * half + 2, :, :].rearrange("p j g t -> p (j g) t")

            def half_scores(half, jj):
                return scores_of(half)[jj][:, :].rearrange("p (g t) -> p g t", g=G)

            def row_max(half, t):
                dve.wait_ge(s_mm[half], t + 1)
                for jj in range(2):
                    ins = dve.tensor_reduce(mx[:, half, 4 * jj:4 * jj + 4], half_scores(half, jj), AX.X, ALU.max)
                ins.then_inc(max_done[half], 1)

            def subtract_max(half, t, first):
                dve.wait_ge(max_done[half], t + 1)
                if not first:
                    dve.wait_ge(pT_mm, 4 * (t - 1) + 2 + 2 * half)
                for jj in range(2):
                    ins = dve.tensor_tensor(prob[:, 2 * half + jj, :, :], half_scores(half, jj),
                                            mx[:, half, 4 * jj:4 * jj + 4, None].to_broadcast([P, G, P]),
                                            ALU.subtract)
                ins.then_inc(sub_done[half], 1)

            def step(n, par, a, f, c):
                t = 2 * n + par
                if a:
                    if f:
                        dve.wait_ge(yT_mm, t)
                    dve.tensor_scalar(y[:, :], x_sb[:, bass.ds(t, 1), :], mv1[:, bass.ds(t, 1), 0], rs1[:, bass.ds(t, 1)],
                                      ALU.subtract, ALU.mult).then_inc(y_done, 1)
                if f:
                    row_max(1, t - 1)
                    subtract_max(1, t - 1, isinstance(n, int) and n == 0)
                if c:
                    dve.wait_ge(gate_mm, t - 1)
                    dve.tensor_tensor(g_sb[:, :], bank[6][:, 0:E], gb_sb[:, :], ALU.add).then_inc(g_done, 1)
                    dve.wait_ge(g_done, t - 1)
                    if not (isinstance(n, int) and n == 1 and par == 0):
                        dve.wait_ge(ew_done, t - 2)
                    dve.sem_inc(dve_turn, 1)
                    dve.max(top[:, :], g_sb[:, :]).then_inc(top_done, 1)
                    dve.wait_ge(top_done, t - 1)
                    dve.tensor_scalar(ntop[:, :], top[:, 0:1], -1.0, None, ALU.mult).then_inc(ntop_done, 1)
                    dve.max_index(topi[:, :], top[:, :], g_sb[:, :]).then_inc(topi_done, 1)
                    dve.wait_ge(topi_done, t - 1)
                    dve.tensor_tensor(hot[:, :, :], cst[:, None, C_IOTA:C_IOTA + E].to_broadcast([P, K, E]),
                                      topi[:, 0:K, None].to_broadcast([P, K, E]), ALU.is_equal).then_inc(hot_done, 1)
                    dve.wait_ge(hot_done, t - 1)
                    if not (isinstance(n, int) and n == 1 and par == 0):
                        dve.wait_ge(msum_done, t - 2)
                    with nc.allow_low_precision(reason="sums of at most four zeros and ones are exact"):
                        dve.tensor_reduce(m_bf[:, :], hot[:, :, :].rearrange("p k e -> p e k"), AX.X,
                                          ALU.add).then_inc(m_done, 1)
                    dve.wait_ge(rank_mm, t - 1)
                    dve.tensor_tensor(place[:, :], bank[7][:, 0:E], cst[:, C_BASE:C_BASE + E],
                                      ALU.add).then_inc(place_done, 1)
                    dve.wait_ge(place_done, t - 1)
                    dve.tensor_tensor(pl_hot[:, :, :], hot[:, :, :], place[:, None, :].to_broadcast([P, K, E]),
                                      ALU.mult).then_inc(plhot_done, 1)
                    dve.wait_ge(plhot_done, t - 1)
                    if not (isinstance(n, int) and n == 1):
                        dve.wait_ge(sent[par], 16 * K * (n - 1))
                    with nc.allow_low_precision(reason="row numbers below 2**15 are exact"):
                        dve.tensor_reduce(pos[:, par, :], pl_hot[:, :, :], AX.X, ALU.add).then_inc(pos_done, 1)
                if a:
                    dve.wait_ge(v_mm, t + 1)
                    if not (isinstance(n, int) and n == 0):
                        dve.wait_ge(pv_mm, t - 1)
                    dve.tensor_tensor(v_ext[:, par, :, 0:DK], bank[6][:, 0:D].rearrange("p (h d) -> p h d", h=H),
                                      bv_sb[:, :].rearrange("p (h d) -> p h d", h=H), ALU.add).then_inc(v_done, 1)
                    row_max(0, t)
                if f:
                    o4 = bank[6][:, :].rearrange("p (g j d) -> p g j d", g=G, j=G)
                    o16 = bank[6][:, :].rearrange("p (h d) -> p h d", h=H)
                    dve.wait_ge(o_mm, t)
                    dve.reciprocal(rden[:, :, :, :].rearrange("p g j o -> p (g j) o"), o16[:, :, DK:DK + 1]).then_inc(rden_done, 1)
                    dve.wait_ge(rden_done, t)
                    dve.tensor_tensor(on[:, :].rearrange("p (h d) -> p h d", h=H), o16[:, :, 0:DK],
                                      rden[:, :, :, :].rearrange("p g j o -> p (g j) o").to_broadcast([P, H, DK]),
                                      ALU.mult).then_inc(on_done, 1)
                if a:
                    subtract_max(0, t, isinstance(n, int) and n == 0 and par == 0)
                if f:
                    dve.wait_ge(wo_mm, t)
                    dve.tensor_tensor(x2[:, bass.ds(t - 1, 1), :], bank[6][:, 0:D], xbo[:, bass.ds(t - 1, 1), :],
                                      ALU.add).then_inc(x2_done, 1)
                if c:
                    dve.wait_ge(ew_done, t - 1)
                if f:
                    dve.wait_ge(x2_done, t)
                if c:
                    dve.reciprocal(rsw[:, :], sw[:, :]).then_inc(rsw_done, 1)
                if f:
                    dve.bn_stats(st2[:, :], x2[:, bass.ds(t - 1, 1), :]).then_inc(st2_done, 1)
                    dve.wait_ge(st2_done, t)
                if c:
                    dve.wait_ge(rsw_done, t - 1)
                    dve.tensor_scalar(w_all[:, bass.ds(t - 2, 1), :], ew[:, :], rsw[:, 0:1], None,
                                      ALU.mult).then_inc(w_done, 1)
                if f:
                    dve.bn_aggr(mv2[:, :], st2[:, :]).then_inc(mv2_done, 1)
                    dve.wait_ge(mv2_done, t)
                    dve.tensor_scalar(ve2[:, 0:1], mv2[:, 1:2], 1.0 + EPS, EPS * EPS, ALU.mult, ALU.add)
                    dve.tensor_scalar(ve2[:, 1:2], mv2[:, 1:2], EPS, None, ALU.add).then_inc(ve2_done, 1)
                    dve.scalar_tensor_tensor(out=tmp[:, :], in0=x2[:, bass.ds(t - 1, 1), :], scalar=mv2[:, 0:1],
                                             in1=sc_sb[:, :], op0=ALU.subtract, op1=ALU.mult).then_inc(tmp_done, 1)
                    dve.wait_ge(tmp_done, t)
                    dve.wait_ge(rs2_done, t)
                    if not (isinstance(n, int) and (n == 0 or (n == 1 and par == 0))):
                        dve.wait_ge(sent[1 - par], 16 * K * (n if par == 1 else n - 1))
                    dve.wait_ge(pool_set, 5)
                    dve.tensor_scalar(rows[:, 1 - par, 0, 0:D], tmp[:, :], rs2[:, 0:1], None, ALU.mult).then_inc(t_done, 1)
                    if not (first(n) and par == 1):
                        dve.wait_ge(xr_done, t - 1)
                    dve.tensor_scalar(z[:, :], x2[:, bass.ds(t - 1, 1), :], mv2[:, 0:1], rs2[:, 1:2],
                                      ALU.subtract, ALU.mult).then_inc(z_done, 1)

            steps(step, dve)

            dve.wait_ge(cnt_mm, 1)
            dve.tensor_copy(cnt[:, :], bank[7][0:TILES, 0:E]).then_inc(plan_step, 1)
            dve.wait_ge(plan_step, 1)
            dve.tensor_tensor(over[:, :, :], cnt[:, :, None].to_broadcast([TILES, E, B]),
                              cst[0:TILES, None, C_STEP:C_STEP + B].to_broadcast([TILES, E, B]),
                              ALU.is_gt).then_inc(plan_step, 1)
            dve.wait_ge(plan_step, 2)
            dve.tensor_reduce(nt[:, :], over[:, :, :], AX.X, ALU.add).then_inc(plan_step, 1)
            dve.wait_ge(plan_step, 3)
            dve.tensor_tensor_scan(incl[:, :], ones_e[:, :], nt[:, :], 0.0, ALU.mult, ALU.add).then_inc(plan_step, 1)
            dve.wait_ge(plan_step, 4)
            dve.tensor_tensor(excl[:, :], incl[:, :], nt[:, :], ALU.subtract).then_inc(plan_step, 1)
            dve.tensor_scalar(past[:, :], incl[:, :], cst[0:TILES, C_P:C_P + 1], None, ALU.is_le).then_inc(plan_step, 1)
            dve.wait_ge(plan_step, 6)
            dve.tensor_reduce(ecol[:, :], past[:, :], AX.X, ALU.add).then_inc(plan_step, 1)
            dve.wait_ge(plan_step, 7)
            dve.tensor_scalar(plan[:, 0:1], ecol[:, :], float(E - 1), None, ALU.min).then_inc(plan_step, 1)
            dve.wait_ge(plan_step, 8)
            dve.tensor_scalar(e_hot[:, :], cst[0:TILES, C_IOTA:C_IOTA + E], plan[:, 0:1], None,
                              ALU.is_equal).then_inc(plan_step, 1)
            dve.wait_ge(plan_step, 9)
            dve.tensor_tensor_reduce(out=junk[:, 0, :], in0=e_hot[:, :], in1=excl[:, :], scale=1.0, scalar=0.0,
                                     op0=ALU.mult, op1=ALU.add, accum_out=base_i[:, :]).then_inc(plan_step, 1)
            dve.tensor_tensor_reduce(out=junk[:, 1, :], in0=e_hot[:, :], in1=cnt[:, :], scale=1.0, scalar=0.0,
                                     op0=ALU.mult, op1=ALU.add, accum_out=cnt_i[:, :]).then_inc(plan_step, 1)
            dve.wait_ge(plan_step, 11)
            dve.tensor_scalar(a_i[:, :], base_i[:, :], cst[0:TILES, C_P:C_P + 1], -float(P), ALU.subtract,
                              ALU.mult).then_inc(plan_step, 1)
            dve.tensor_scalar(m_i[:, :], cnt_i[:, :], -float(P), 0.0, ALU.add, ALU.max).then_inc(plan_step, 1)
            dve.wait_ge(plan_step, 13)
            dve.tensor_tensor(r0_i[:, :], a_i[:, :], m_i[:, :], ALU.min).then_inc(plan_step, 1)
            dve.wait_ge(plan_step, 14)
            dve.scalar_tensor_tensor(out=plan[:, 1:2], in0=plan[:, 0:1], scalar=float(TOK), in1=r0_i[:, :],
                                     op0=ALU.mult, op1=ALU.add).then_inc(plan_step, 1)
            dve.tensor_tensor(plan[:, 2:3], a_i[:, :], r0_i[:, :], ALU.subtract).then_inc(plan_step, 1)
            dve.tensor_tensor(plan[:, 3:4], cnt_i[:, :], r0_i[:, :], ALU.subtract).then_inc(plan_step, 1)
            dve.wait_ge(plan_step, 17)
            dve.tensor_tensor(diag[:, :, :], cst[0:TILES, None, C_ID:C_ID + TILES].to_broadcast([TILES, 4, TILES]),
                              plan[:, :, None].to_broadcast([TILES, 4, TILES]), ALU.mult).then_inc(diag_done, 1)
            dve.wait_ge(plan_mm, 1)
            dve.tensor_copy(tab[:, :, :], bank[6][0:1, 0:2 * TILES].rearrange("p (a i) -> p a i", a=2)).then_inc(tab_done, 1)
            dve.tensor_scalar(inv[:, 0, :], bank[6][:, 2 * TILES:3 * TILES], cst[:, C_P:C_P + 1], None, ALU.is_gt)
            dve.tensor_scalar(inv[:, 1, :], bank[6][:, 3 * TILES:4 * TILES], cst[:, C_P:C_P + 1], None,
                              ALU.is_le).then_inc(inv_done, 1)
            dve.wait_ge(inv_done, 1)
            dve.tensor_tensor(inv[:, 2, :], inv[:, 0, :], inv[:, 1, :], ALU.max).then_inc(inv_done, 1)
            dve.wait_ge(inv_done, 2)
            dve.tensor_tensor(aside[:, :], inv[:, 2, :], cst[:, C_DUMMY:C_DUMMY + TILES], ALU.mult).then_inc(aside_done, 1)
            dve.wait_ge(aside_done, 1)

            def pstep(n, par, xin, work, mid, end):
                q = 2 * n + par
                if end:
                    dve.wait_ge(code_done, q - 1)
                    if not (isinstance(n, int) and n < 2):
                        dve.wait_ge(back[par], 32 * (n - 1))
                    dve.tensor_copy(dest[:, par, :], dest_all[:, bass.ds(4 * (n - 1) + 2 * par, 2)]).then_inc(dest_done, 1)
                if work:
                    hb = bank[par][:, :].rearrange("p (i f) -> p i f", i=2)
                    dve.wait_ge(xt_ld[par], 32 * n + 32)
                    dve.tensor_tensor(dest_all[:, bass.ds(4 * n + 2 * par, 2)], xt[:, par, :, D],
                                      aside[:, bass.ds(4 * n + 2 * par, 2)], ALU.max).then_inc(code_done, 1)
                    dve.wait_ge(h_mm, q + 1)
                    dve.tensor_scalar(glu[:, par, :, :], hb[:, :, 0:FF], LIMIT, None, ALU.min).then_inc(glu_done, 1)
                    dve.tensor_scalar(lin[:, par, :, :], hb[:, :, FF:2 * FF], LIMIT, -LIMIT, ALU.min,
                                      ALU.max).then_inc(lin_done, 1)
                    dve.wait_ge(sg_done, q + 1)
                    dve.tensor_tensor(gs[:, par, :, :], glu[:, par, :, :], sg[:, par, :, :], ALU.mult).then_inc(gs_done, 1)
                    dve.wait_ge(gs_done, q + 1)
                    if not (isinstance(n, int) and n == 0):
                        dve.wait_ge(hidT_mm, q - 1)
                    dve.scalar_tensor_tensor(out=hid[:, par, :, :], in0=lin[:, par, :, :], scalar=1.0,
                                             in1=gs[:, par, :, :], op0=ALU.add, op1=ALU.mult).then_inc(hid_done, 1)

            pair_steps(pstep, dve)

            dve.wait_ge(w_done, B)
            dve.wait_ge(xr_done, B)
            for b in range(B):
                dve.wait_ge(fin_ld[b], 16)
                for k in range(K):
                    if k:
                        dve.wait_ge(acc_done, K * b + k)
                    dve.scalar_tensor_tensor(out=acc[:, b, :], in0=fin[:, b, k, :], scalar=w_all[:, b, k:k + 1],
                                             in1=xr[:, b, :] if k == 0 else acc[:, b, :],
                                             op0=ALU.mult, op1=ALU.add).then_inc(acc_done, 1)


def kernel(x, ctx_1024, L0_xattn_wq, L0_xattn_bq, L0_xattn_wk, L0_xattn_bk, L0_xattn_wv, L0_xattn_bv,
           L0_xattn_wo, L0_xattn_bo, L0_ffn_norm_scale, L0_ffn_gate_w, L0_ffn_gate_b, L0_ffn_w1, L0_ffn_b1,
           L0_ffn_w2, L0_ffn_b2):
    import concourse.bacc as bacc
    from concourse.bass_utils import run_bass_kernel_spmd

    def padded(w):
        r = np.zeros((D, G, G, 32), np.float32)
        r[:, :, :, 0:DK] = np.asarray(w).T.reshape(D, G, G, DK)
        return r.reshape(D, G, P)

    def padded_bias(b):
        r = np.zeros((G, G, 32), np.float32)
        r[:, :, 0:DK] = np.asarray(b).reshape(G, G, DK)
        return np.ascontiguousarray(r.reshape(G, P).T)

    w1 = np.asarray(L0_ffn_w1).reshape(E, FF, 2, D)
    b1 = np.asarray(L0_ffn_b1).reshape(E, FF, 2).transpose(0, 2, 1).reshape(P, -1)
    b2 = np.asarray(L0_ffn_b2).reshape(P, -1)
    arrays = {
        "x": np.asarray(x).reshape(TOK, D),
        "ctxT": np.asarray(ctx_1024).reshape(TOK, D).T,
        "wq": padded(L0_xattn_wq), "bq": padded_bias(L0_xattn_bq),
        "wk": padded(L0_xattn_wk), "bk": padded_bias(L0_xattn_bk),
        "wvT": np.asarray(L0_xattn_wv).T, "bv": np.asarray(L0_xattn_bv).reshape(1, D),
        "woT": np.asarray(L0_xattn_wo).T, "bo": np.asarray(L0_xattn_bo).reshape(1, D),
        "scale": np.asarray(L0_ffn_norm_scale).reshape(1, D),
        "gateT": np.asarray(L0_ffn_gate_w).T, "gate_b": np.asarray(L0_ffn_gate_b).reshape(1, E),
        "w1T": w1.transpose(3, 0, 2, 1).reshape(D, E, 2 * FF),
        "w2T": np.asarray(L0_ffn_w2).transpose(2, 0, 1),
        "b12": np.concatenate([b1, b2], axis=1),
        "consts": shape_constants(),
    }
    arrays = {k: np.ascontiguousarray(v) for k, v in arrays.items()}
    nc = bacc.Bacc("TRN2", target_bir_lowering=False, num_devices=1)
    args = {k: nc.dram_tensor(f"in_{k}", v.shape, mybir.dt.from_np(v.dtype), kind="ExternalInput").ap()
            for k, v in arrays.items()}
    out = nc.dram_tensor("out_0", (TOK, D), F32, kind="ExternalOutput").ap()
    build(nc, out=out, **args)
    r = run_bass_kernel_spmd(nc, [{f"in_{k}": v for k, v in arrays.items()}], core_ids=[0])
    return r.results[0]["out_0"].reshape(B, P, D)
```

```python
from contextlib import ExitStack

import numpy as np

import concourse.bass as bass
from concourse import mybir

F32 = mybir.dt.float32
BF16 = mybir.dt.bfloat16
I32 = mybir.dt.int32
U32 = mybir.dt.uint32
ALU = mybir.AluOpType
ACT = mybir.ActivationFunctionType
AX = mybir.AxisListType

P = 128
B = 8
D = 128
H = 16
DK = D // H
G = 4
HP = H // 2
E = 32
K = 4
FF = 128
TOK = B * P
TILES = 64
PAIRS = TILES // 2
ACT_ROWS = 2
U = 4
ROW = D + 4
LIMIT = 7.0
ALPHA = 1.702
EPS = 1e-5

C_ID, C_TRI, C_IOTA, C_BASE, C_CODE, C_P, C_DUMMY, C_STEP = 0, 128, 256, 288, 320, 352, 353, 417
C_PAIR = C_STEP + B
C_END = C_PAIR + 1
NB = 3 * D


def shape_constants():
    c = np.zeros((P, C_END), np.float32)
    p = np.arange(P)
    c[:, C_ID:C_ID + P] = np.eye(P)
    c[:, C_TRI:C_TRI + P] = p[:, None] < p[None, :]
    c[:, C_IOTA:C_IOTA + E] = np.arange(E)
    c[:, C_BASE:C_BASE + E] = TOK * np.arange(E)
    b, k = np.meshgrid(np.arange(B), np.arange(K), indexing="ij")
    c[:, C_CODE:C_CODE + B * K] = (k * TOK + b * P).reshape(-1)[None, :] + p[:, None]
    c[:, C_P] = p
    c[:, C_DUMMY:C_DUMMY + TILES] = K * TOK + P * np.arange(TILES)[None, :] + p[:, None]
    c[:, C_STEP:C_STEP + B] = P * np.arange(B)
    c[:, C_PAIR] = np.where(p % 64 < 24, p % 8, -1)
    return c


def build(nc, x, ctxT, wqT, wkvT, small_b, woT, bo, scale, gateT, gate_b, w1T, w2T, b12, consts, out):
    ctx = ExitStack()

    def sb(name, shape, dt=F32):
        return ctx.enter_context(nc.sbuf_tensor(name, shape, dt))

    def sem(name):
        return ctx.enter_context(nc.semaphore(name))

    with ctx:
        routed = nc.dram_tensor("routed", (E * TOK, ROW), F32, kind="Internal").ap()
        returned = nc.dram_tensor("returned", (K * TOK + TILES * P, D), F32, kind="Internal").ap()
        bias_d = nc.dram_tensor("bias_parts", (3, P * 96), BF16, kind="Internal").ap()

        x_sb = sb("x_sb", [P, B, D])
        xbo = sb("xbo", [P, B, D])
        cT_all = sb("cT_all", [P, B, P])
        yT_all = sb("yT_all", [P, B, P])
        yc = sb("yc", [P, 2, 2, P])
        wq_sb = sb("wq_sb", [P, D])
        wkv_sb = sb("wkv_sb", [P, 2 * D])
        wo_sb = sb("wo_sb", [P, D])
        bo_sb = sb("bo_sb", [P, D])
        sc_sb = sb("sc_sb", [P, D])
        gate_sb = sb("gate_sb", [P, E])
        gb_sb = sb("gb_sb", [P, E])
        g_sb = sb("g_sb", [P, E])
        cst = sb("cst", [P, C_END])
        w1_sb = sb("w1_sb", [P, E, 2 * FF])
        w2_sb = sb("w2_sb", [P, E, D])
        b_sb = sb("b_sb", [P, 96])
        b_res = sb("b_res", [P, 2, 96])
        b_part = sb("b_part", [P, 3, 96], BF16)
        bias_rows = sb("bias_rows", [3, P * 96], BF16)
        sb_row = sb("sb_row", [1, NB])
        sb_res = sb("sb_res", [1, 2, NB])
        sb_part = sb("sb_part", [1, 3, NB], BF16)
        small_rows = sb("small_rows", [3, NB], BF16)
        tri_bf = sb("tri_bf", [P, P], BF16)
        id_bf = sb("id_bf", [P, P], BF16)
        sel = sb("sel", [P, HP, P], BF16)
        ones_bf = sb("ones_bf", [P, P], BF16)
        ones_f = sb("ones_f", [P, P])
        zeros = sb("zeros", [P, ROW])
        ident = cst[:, C_ID:C_ID + P]
        st1 = sb("st1", [P, B, 6])
        mv1 = sb("mv1", [P, B, 2])
        ve1 = sb("ve1", [P, B])
        rs1 = sb("rs1", [P, B])
        half_neg = sb("half_neg", [P, B])
        y_all = sb("y_all", [P, B, D])
        parts = sb("parts", [P, 2, H, 8, DK], BF16)
        res = sb("res", [P, 2, H, DK])
        qk_sb = sb("qk_sb", [P, 2, 2, HP, P], BF16)
        v_ext = sb("v_ext", [P, 2, H, 32])
        table_ahead = sb("table_ahead", [P, 1])
        mx = sb("mx", [P, 2, HP])
        mx_res = sb("mx_res", [P, 2, HP])
        mx_part = sb("mx_part", [P, 2, 64], BF16)
        mT_sb = sb("mT_sb", [P, P], BF16)
        pT = sb("pT", [P, 2, 2, HP // 2, P])
        oT = sb("oT", [P, G, P])
        rden = sb("rden", [P, H, 1])
        on = sb("on", [P, D])
        onT = sb("onT", [P, P])
        x2 = sb("x2", [P, B, D])
        st2 = sb("st2", [P, 6])
        mv2 = sb("mv2", [P, 2])
        ve2 = sb("ve2", [P, 1])
        rs2 = sb("rs2", [P, 1])
        xr = sb("xr", [P, B, D])
        st3 = sb("st3", [P, B, 6])
        mv3 = sb("mv3", [P, B, 2])
        ve3 = sb("ve3", [P, B])
        rs3 = sb("rs3", [P, B])
        a3 = sb("a3", [P, B])
        c3 = sb("c3", [P, B])
        tmp = sb("tmp", [P, D])
        rows = sb("rows", [P, 2, K, ROW])
        tT = sb("tT", [P, P])
        top = sb("top", [P, 8])
        topi = sb("topi", [P, 8], U32)
        top_all = sb("top_all", [P, B, K])
        ew = sb("ew", [P, B, K])
        sw = sb("sw", [P, B])
        rsw = sb("rsw", [P, B])
        w_all = sb("w_all", [P, B, K])
        hot = sb("hot", [P, K, E])
        m_bf = sb("m_bf", [P, E], BF16)
        m_sum = sb("m_sum", [P, E], BF16)
        place = sb("place", [P, E])
        pl_hot = sb("pl_hot", [P, K, E])
        pos = sb("pos", [P, 2, K], U32)
        cnt = sb("cnt", [TILES, E])
        over = sb("over", [TILES, E, B])
        nt = sb("nt", [TILES, E])
        ones_e = sb("ones_e", [TILES, E])
        incl = sb("incl", [TILES, E])
        excl = sb("excl", [TILES, E])
        past = sb("past", [TILES, E])
        plan = sb("plan", [TILES, 4])
        ecol = sb("ecol", [TILES, 1])
        e_hot = sb("e_hot", [TILES, E])
        junk = sb("junk", [TILES, 2, E])
        base_i = sb("base_i", [TILES, 1])
        cnt_i = sb("cnt_i", [TILES, 1])
        a_i = sb("a_i", [TILES, 1])
        m_i = sb("m_i", [TILES, 1])
        r0_i = sb("r0_i", [TILES, 1])
        diag = sb("diag", [TILES, 4, TILES])
        tab = sb("tab", [1, 2, TILES], I32)
        inv = sb("inv", [P, 3, TILES])
        aside = sb("aside", [P, TILES])
        xt = sb("xt", [P, U, 2, ROW])
        xtT = sb("xtT", [P, 2, 2, P])
        glu = sb("glu", [P, 2, 2, FF])
        lin = sb("lin", [P, 2, 2, FF])
        sg = sb("sg", [P, 2, 2, FF])
        gs = sb("gs", [P, 2, 2, FF])
        hid = sb("hid", [P, 2, 2, FF])
        hidT = sb("hidT", [P, 2, 2, P])
        y_sb = sb("y_sb", [P, U, 2, D])
        dest = sb("dest", [P, U, 2], U32)
        dest_all = sb("dest_all", [P, TILES], U32)
        fin = sb("fin", [P, B, K, D])
        acc = y_all
        weighed_sb = sb("weighed_sb", [P, ACT_ROWS, K, D])
        half_sum = yT_all[:, 0:2 * ACT_ROWS, :].rearrange("p (b k) d -> p b k d", b=ACT_ROWS)
        part_sum = cT_all[:, 0:ACT_ROWS, :]

        scores = [ctx.enter_context(nc.psum_tensor(f"scores{i}", [P, 1024], F32)) for i in range(2)]
        bank = [scores[0][:, 0:512], scores[0][:, 512:1024], scores[1][:, 0:512], scores[1][:, 512:1024]]
        bank += [ctx.enter_context(nc.psum_tensor(f"bank{i}", [P, 512], F32))[:, :] for i in range(4, 8)]
        turned = [bank[4].bitcast(BF16), bank[5].bitcast(BF16)]
        m_turned = bank[7][:, 0:P // 2].bitcast(BF16)
        g_ps = bank[4][:, 0:E]
        rank_ps = bank[4][:, E:2 * E]

        cst_ld = sem("cst_ld")
        sbias_ld = sem("sbias_ld")
        wqkv_ld = sem("wqkv_ld")
        ln_ld = sem("ln_ld")
        wo_ld = sem("wo_ld")
        ffw_ld = sem("ffw_ld")
        bias_ld = sem("bias_ld")
        zero_set = sem("zero_set")
        filled = sem("filled")
        const_set = sem("const_set")
        pool_set = sem("pool_set")
        st1_done = sem("st1_done")
        mv1_done = sem("mv1_done")
        pool_turn = sem("pool_turn")
        dve_turn = sem("dve_turn")
        ve1_done = sem("ve1_done")
        rs1_done = sem("rs1_done")
        xbo_done = sem("xbo_done")
        ssplit = sem("ssplit")
        sbias_out = sem("sbias_out")
        bsplit = sem("bsplit")
        bias_out = sem("bias_out")
        y_done = sem("y_done")
        yT_mm = sem("yT_mm")
        yT_done = sem("yT_done")
        proj_mm = sem("proj_mm")
        p1_done = sem("p1_done")
        v_done = sem("v_done")
        r1_done = sem("r1_done")
        p2_done = sem("p2_done")
        kpart_done = sem("kpart_done")
        qpart_done = sem("qpart_done")
        k_mm = sem("k_mm")
        q_mm = sem("q_mm")
        k_done = sem("k_done")
        q_done = sem("q_done")
        x_ld = [sem("x_ld0"), sem("x_ld1")]
        c_ld = [sem("c_ld0"), sem("c_ld1")]
        yc_ld = [sem("yc_ld0"), sem("yc_ld1")]
        s_mm = [sem("s_mm0"), sem("s_mm1")]
        st_mm = [sem("st_mm0"), sem("st_mm1")]
        exp_done = [sem("exp_done0"), sem("exp_done1")]
        max_done = sem("max_done")
        neg_done = sem("neg_done")
        mres_done = sem("mres_done")
        mhi_done = sem("mhi_done")
        mpart_done = sem("mpart_done")
        m_turn_mm = sem("m_turn_mm")
        mT_done = sem("mT_done")
        pv_mm = sem("pv_mm")
        oT_done = sem("oT_done")
        o_mm = sem("o_mm")
        rden_done = sem("rden_done")
        on_done = sem("on_done")
        onT_mm = sem("onT_mm")
        onT_done = sem("onT_done")
        wo_mm = sem("wo_mm")
        x2_done = sem("x2_done")
        st2_done = sem("st2_done")
        mv2_done = sem("mv2_done")
        ve2_done = sem("ve2_done")
        rs2_done = sem("rs2_done")
        tmp_done = sem("tmp_done")
        code_set = sem("code_set")
        t_done = sem("t_done")
        tT_mm = sem("tT_mm")
        tT_done = sem("tT_done")
        gate_mm = sem("gate_mm")
        g_done = sem("g_done")
        top_done = sem("top_done")
        topi_done = sem("topi_done")
        keep_done = sem("keep_done")
        hot_done = sem("hot_done")
        m_done = sem("m_done")
        rank_mm = sem("rank_mm")
        msum_done = sem("msum_done")
        place_done = sem("place_done")
        plhot_done = sem("plhot_done")
        pos_done = sem("pos_done")
        st3_done = sem("st3_done")
        mv3_done = sem("mv3_done")
        ve3_done = sem("ve3_done")
        rs3_done = sem("rs3_done")
        a3_done = sem("a3_done")
        xr_done = sem("xr_done")
        wsub_done = sem("wsub_done")
        ew_done = sem("ew_done")
        sw_done = sem("sw_done")
        rsw_done = sem("rsw_done")
        w_done = sem("w_done")
        sent = [sem("sent0"), sem("sent1")]
        sent_rows = [sem("sent_rows0"), sem("sent_rows1")]
        cnt_mm = sem("cnt_mm")
        plan_step = sem("plan_step")
        diag_done = sem("diag_done")
        plan_mm = sem("plan_mm")
        tab_done = sem("tab_done")
        inv_done = sem("inv_done")
        aside_done = sem("aside_done")
        xt_ld = [sem(f"xt_ld{i}") for i in range(U)]
        xtT_mm = sem("xtT_mm")
        xtT_done = sem("xtT_done")
        h_mm = sem("h_mm")
        glu_done = sem("glu_done")
        lin_done = sem("lin_done")
        sg_done = sem("sg_done")
        gs_done = sem("gs_done")
        hid_done = sem("hid_done")
        hidT_mm = sem("hidT_mm")
        hidT_done = sem("hidT_done")
        y_mm = sem("y_mm")
        ysb_done = sem("ysb_done")
        dest_done = sem("dest_done")
        code_done = sem("code_done")
        back = [sem(f"back{i}") for i in range(U)]
        fin_ld = [sem(f"fin_ld{b}") for b in range(B)]
        weighed = sem("weighed")
        half_sum_done = sem("half_sum_done")
        part_sum_done = sem("part_sum_done")
        acc_done = [sem(f"acc_done{b}") for b in range(B)]
        out_st = sem("out_st")

        block = ctx.enter_context(nc.Block())

        def steps(fn, engine):
            fn(0, 0, True, False, False, True)
            fn(0, 1, True, True, False, True)
            with engine.Fori(1, B // 2 - 1) as n:
                fn(n, 0, True, True, True, True)
                fn(n, 1, True, True, True, True)
            fn(B // 2 - 1, 0, True, True, True, True)
            fn(B // 2 - 1, 1, True, True, True, False)
            fn(B // 2, 0, False, True, True, False)
            fn(B // 2, 1, False, False, True, False)

        def pair_steps(fn, engine):
            for i in range(U):
                fn(0, i, True, True, i >= 2, i >= 3)
            for i in range(U):
                fn(1, i, True, True, True, True)
            with engine.Fori(2, PAIRS // U - 1) as n:
                for i in range(U):
                    fn(n, i, True, True, True, True)
            for i in range(U):
                fn(PAIRS // U - 1, i, i < U - 1, True, True, True)
            for i in range(3):
                fn(PAIRS // U, i, False, False, i < 2, True)

        def from_slot(n, i, q):
            return not isinstance(n, int) or U * n + i >= q

        def table(engine, kind, row, start, count, top):
            _, vals = nc.values_load_multi_w_load_instructions(
                tab[0:1, row, bass.ds(start, count)], engines=(kind,), min_val=0, max_val=top,
                skip_runtime_bounds_check_because="the plan clamps the expert to E-1 and the row to the expert's")
            return list(vals)

        def weighted_sum(engine, bs):
            engine.wait_ge(w_done, 1)
            engine.wait_ge(xr_done, B)
            for k in range(K):
                for b in bs:
                    if k:
                        engine.wait_ge(acc_done[b], k)
                    else:
                        engine.wait_ge(fin_ld[b], 16)
                    engine.scalar_tensor_tensor(out=acc[:, b, :], in0=fin[:, b, k, :], scalar=w_all[:, b, k:k + 1],
                                                in1=acc[:, b, :] if k else xr[:, b, :],
                                                op0=ALU.mult, op1=ALU.add).then_inc(acc_done[b], 1)

        @block.sync
        def _(sp):
            sp.dma_start(sb_row[:, :], small_b).then_inc(sbias_ld, 16)
            x_rows = x.rearrange("(b p) d -> p b d", p=P)
            ctx_rows = ctxT.rearrange("i (b t) -> i b t", b=B)
            sp.dma_start(x_sb[:, 0:4, :], x_rows[:, 0:4]).then_inc(x_ld[0], 16)
            sp.dma_start(x_sb[:, 4:8, :], x_rows[:, 4:8]).then_inc(x_ld[1], 16)
            sp.dma_start(cst[:, :], consts).then_inc(cst_ld, 16)
            sp.dma_start(wkv_sb[:, :], wkvT).then_inc(wqkv_ld, 16)
            sp.dma_start(wq_sb[:, :], wqT).then_inc(wqkv_ld, 16)
            sp.dma_start(cT_all[:, 0:2, :], ctx_rows[:, 0:2]).then_inc(c_ld[0], 16)
            sp.wait_ge(ssplit, 5)
            sp.dma_start(small_rows[:, :], sb_part[0:1, :, :]).then_inc(sbias_out, 16)
            sp.dma_start(cT_all[:, 2:8, :], ctx_rows[:, 2:8]).then_inc(c_ld[1], 16)
            sp.dma_start(wo_sb[:, :], woT).then_inc(wo_ld, 16)
            sp.dma_start(gate_sb[:, :], gateT).then_inc(wo_ld, 16)
            sp.dma_start(b_sb[:, :], b12).then_inc(bias_ld, 16)
            sp.wait_ge(zero_set, 1)
            sp.dma_start(routed.rearrange("(e r) c -> r e c", e=E)[0:P],
                         zeros[:, None, :].to_broadcast([P, E, ROW])).then_inc(filled, 16)
            sp.wait_ge(c_ld[1], 16)
            sp.wait_ge(yT_done, 2)
            def load_row(r):
                sp.dma_start(yc[:, r % 2, 0, :], yT_all[:, r, :]).then_inc(yc_ld[r % 2], 16)
                sp.dma_start(yc[:, r % 2, 1, :], cT_all[:, r, :]).then_inc(yc_ld[r % 2], 16)

            def count_sent(r):
                sp.wait_ge(sent[r % 2], 16 * K * (r // 2 + 1))
                sp.sem_inc(sent_rows[r % 2], 1)

            load_row(3)
            load_row(4)
            for b in range(B):
                if b in (5, 6):
                    sp.wait_ge(proj_mm, b - 1)
                    load_row(b)
                    count_sent(b - 5)
                e0, e1 = b * E // B, (b + 1) * E // B
                sp.dma_start(w1_sb[:, e0:e1, :], w1T[:, e0:e1, :]).then_inc(ffw_ld, 16)
                sp.dma_start(w2_sb[:, e0:e1, :], w2T[:, e0:e1, :]).then_inc(ffw_ld, 16)
                if b == 3:
                    sp.wait_ge(bsplit, 5)
                    sp.dma_start(bias_d[:, 0:P * 64].rearrange("r (p c) -> p r c", p=P), b_part[:, :, 0:64]).then_inc(bias_out, 16)
                    sp.dma_start(bias_d[:, P * 64:].rearrange("r (p c) -> p r c", p=P), b_part[:, :, 64:96]).then_inc(bias_out, 16)
                if b == B - 1:
                    sp.wait_ge(bias_out, 32)
                    sp.dma_start(bias_rows[:, :], bias_d).then_inc(bias_out, 16)
            for r in range(2, B - 2):
                count_sent(r)

            sp.wait_ge(tab_done, 1)
            for par in range(2):
                sp.wait_ge(sent[par], 16 * K * (B // 2))

            def load_pairs(n, again):
                for i in range(U):
                    if i % 2 == 0:
                        r = table(sp, mybir.EngineType.SP, 1, 2 * U * n + 2 * i, 4, E * TOK - P)
                    if again:
                        sp.wait_ge(xtT_mm, U * n + i - U + 1)
                        sp.wait_ge(code_done, U * n + i - U + 1)
                    for h in range(2):
                        sp.dma_start(xt[:, i, h, :], routed[bass.ds(r[2 * (i % 2) + h], P), :]).then_inc(xt_ld[i], 16)

            load_pairs(0, False)
            with sp.Fori(1, PAIRS // U) as n:
                load_pairs(n, True)

            for i in range(U):
                sp.wait_ge(back[i], 32 * (PAIRS // U))
            order = (2, 0, 3, 1, 4, 5, 6, 7)
            for b in order:
                src = returned[0:K * TOK, :].rearrange("(k b p) d -> b p k d", k=K, p=P)
                sp.dma_start(fin[:, b, :, :], src[b]).then_inc(fin_ld[b], 16)
            for b in (2, 3, 4, 0, 1, 5, 6, 7):
                sp.wait_ge(acc_done[b], K)
                sp.dma_start(out[b * P:(b + 1) * P, :], acc[:, b, :]).then_inc(out_st, 16)
            sp.wait_ge(out_st, 16 * B)

        @block.gpsimd
        def _(pool):
            pool.memset(zeros[:, :], 0.0).then_inc(zero_set, 1)
            pool.memset(half_neg[:, :], -0.5).then_inc(pool_set, 1)
            pool.memset(v_ext[:, :, :, :], 0.0).then_inc(pool_set, 1)
            pool.memset(mx_part[:, :, :], 0.0).then_inc(pool_set, 1)
            pool.memset(rows[:, :, :, :], 0.0).then_inc(pool_set, 1)
            pool.memset(m_sum[:, :], 0.0).then_inc(msum_done, 1)
            for par in range(2):
                pool.sem_inc(sent_rows[par], 1)
            pool.wait_ge(pool_set, 4)
            pool.memset(v_ext[:, :, :, DK:DK + 1], 1.0).then_inc(pool_set, 1)
            for h in range(2):
                pool.wait_ge(ve1_done, h + 1)
                pool.tensor_tensor(rs1[:, 4 * h:4 * h + 4], ve1[:, 4 * h:4 * h + 4], half_neg[:, 0:4],
                                   ALU.pow).then_inc(rs1_done, 1)
            pool.wait_ge(x_ld[0], 16)
            pool.wait_ge(x_ld[1], 16)
            pool.wait_ge(ln_ld, 48)
            pool.tensor_tensor(xbo[:, :, :], x_sb[:, :, :], bo_sb[:, None, :].to_broadcast([P, B, D]),
                               ALU.add).then_inc(xbo_done, 1)

            def scatter(par, ks):
                for k in ks:
                    pool.indirect_dma_start(
                        out=routed, out_offset=bass.IndirectOffsetOnAxis(ap=pos[:, par, k:k + 1], axis=0),
                        in_=rows[:, par, k, :], in_offset=None).then_inc(sent[par], 16)

            def step(n, par, a, b, c, p):
                t = 2 * n + par
                if c:
                    pool.wait_ge(sent_rows[par], n)
                    pool.sem_inc(pool_turn, 1)
                    code = cst[:, bass.ds(C_CODE + K * (t - 2), K)]
                    pool.tensor_copy(rows[:, par, :, D], code).then_inc(code_set, 1)
                    pool.wait_ge(rank_mm, t - 1)
                    pool.tensor_tensor(m_sum[:, :], m_sum[:, :], m_bf[:, :], ALU.add).then_inc(msum_done, 1)
                    pool.wait_ge(code_set, t - 1)
                    pool.wait_ge(pos_done, t - 1)
                    pool.wait_ge(filled, 16)
                    pool.sem_inc(pool_turn, 1)
                    scatter(par, (0, 1))
                if b:
                    pool.wait_ge(ve2_done, t)
                    pool.tensor_tensor(rs2[:, :], ve2[:, :], half_neg[:, 0:1], ALU.pow).then_inc(rs2_done, 1)
                if c:
                    scatter(par, (2, 3))

            steps(step, pool)

            def pstep(n, i, xin, work, mid, end):
                if end:
                    q, buf = U * n + i, (i + 1) % U
                    pool.wait_ge(ysb_done, q - 2)
                    pool.wait_ge(dest_done, q - 2)
                    pool.sem_inc(pool_turn, 1)
                    for h in range(2):
                        pool.indirect_dma_start(
                            out=returned,
                            out_offset=bass.IndirectOffsetOnAxis(ap=dest[:, buf, h:h + 1], axis=0),
                            in_=y_sb[:, buf, h, :], in_offset=None).then_inc(back[buf], 16)

            pair_steps(pstep, pool)

            pool.wait_ge(ve3_done, 1)
            pool.tensor_tensor(rs3[:, :], ve3[:, :], half_neg[:, :], ALU.pow).then_inc(rs3_done, 1)

            pool.wait_ge(xr_done, B)
            for b in range(ACT_ROWS):
                pool.wait_ge(weighed, b + 1)
                pool.tensor_tensor(half_sum[:, b, :, :], weighed_sb[:, b, 0:2, :], weighed_sb[:, b, 2:4, :],
                                   ALU.add).then_inc(half_sum_done, 1)
            for b in range(ACT_ROWS):
                pool.wait_ge(half_sum_done, b + 1)
                pool.tensor_tensor(part_sum[:, b, :], half_sum[:, b, 0, :], half_sum[:, b, 1, :],
                                   ALU.add).then_inc(part_sum_done, 1)
            for b in range(ACT_ROWS):
                pool.wait_ge(part_sum_done, b + 1)
                pool.tensor_tensor(acc[:, b, :], part_sum[:, b, :], xr[:, b, :], ALU.add).then_inc(acc_done[b], K)

        @block.scalar
        def _(act):
            act.dma_start(bo_sb[:, :], bo.to_broadcast([P, D])).then_inc(ln_ld, 16)
            act.dma_start(sc_sb[:, :], scale.to_broadcast([P, D])).then_inc(ln_ld, 16)
            act.dma_start(gb_sb[:, :], gate_b.to_broadcast([P, E])).then_inc(ln_ld, 16)
            def copy(dst, src):
                return act.activation(dst, src, ACT.Copy)

            for h in range(2):
                act.wait_ge(yT_mm, h + 1)
                copy(yT_all[:, 4 * h:4 * h + 4, :], bank[h]).then_inc(yT_done, 1)

            def project_out(r, par):
                act.wait_ge(proj_mm, r + 1)
                kq = bank[6][:, 0:2 * D].rearrange("p (i h d) -> p i h d", i=2, h=H)
                copy(parts[:, 1, :, 0:7:3, :], kq[:, 1, :, None, :].to_broadcast([P, H, 3, DK]))
                copy(parts[:, 0, :, 0:3, :], kq[:, 0, :, None, :].to_broadcast([P, H, 3, DK])).then_inc(p1_done, 1)
                copy(v_ext[:, par, :, 0:DK],
                     bank[6][:, 2 * D:3 * D].rearrange("p (h d) -> p h d", h=H)).then_inc(v_done, 1)

            def exp_half(half, t):
                act.wait_ge(st_mm[half], t)
                act.activation(pT[:, half, :, :, :], scores[half][:, :].rearrange("p (j i s) -> p j i s", j=2, i=HP // 2),
                               ACT.Exp, scale=float(DK) ** -0.5).then_inc(exp_done[half], 1)

            def step(n, par, a, b, c, p):
                t = 2 * n + par
                if b:
                    act.wait_ge(m_turn_mm, t)
                    copy(mT_sb[:, :], m_turned).then_inc(mT_done, 1)
                if a:
                    act.wait_ge(k_mm, t + 1)
                    copy(qk_sb[:, par, 1, :, :], turned[0].rearrange("p (i s) -> p i s", i=HP)).then_inc(k_done, 1)
                if c:
                    act.wait_ge(tT_mm, t - 1)
                    copy(tT[:, :], bank[6][:, 0:P]).then_inc(tT_done, 1)
                if b:
                    exp_half(0, t)
                    exp_half(1, t)
                    act.wait_ge(pv_mm, t)
                    copy(oT[:, :, :], bank[7]).then_inc(oT_done, 1)
                if p:
                    project_out(t + 1, 1 - par)
                if b:
                    act.wait_ge(onT_mm, t)
                    copy(onT[:, :], bank[5][:, 0:P]).then_inc(onT_done, 1)

            act.wait_ge(pool_set, 5)
            project_out(0, 0)
            steps(step, act)

            act.wait_ge(wsub_done, 1)
            act.activation(ew[:, :, :], ew[:, :, :], ACT.Exp).then_inc(ew_done, 1)
            act.activation(table_ahead[:, :], half_neg[:, 0:1], ACT.Sigmoid)

            def pstep(n, i, xin, work, mid, end):
                q, par = U * n + i, i % 2
                if xin:
                    act.wait_ge(xtT_mm, q + 2)
                    copy(xtT[:, 1 - par, :, :], bank[5 - par][:, 0:2 * P]).then_inc(xtT_done, 1)
                if mid:
                    act.wait_ge(hidT_mm, q - 1)
                    copy(hidT[:, par, :, :], bank[6 + par][:, 0:2 * P]).then_inc(hidT_done, 1)
                if end:
                    buf = (i + 1) % U
                    act.wait_ge(y_mm, q - 2)
                    if from_slot(n, i, U + 3):
                        act.wait_ge(back[buf], 32 * (n if i == U - 1 else n - 1))
                    copy(y_sb[:, buf, :, :], bank[3 - par][:, 0:2 * D]).then_inc(ysb_done, 1)
                if work:
                    act.wait_ge(glu_done, q + 1)
                    act.activation(sg[:, par, :, :], glu[:, par, :, :], ACT.Sigmoid, scale=ALPHA).then_inc(sg_done, 1)

            act.wait_ge(xtT_mm, 1)
            copy(xtT[:, 0, :, :], bank[4][:, 0:2 * P]).then_inc(xtT_done, 1)
            pair_steps(pstep, act)

            act.wait_ge(w_done, 1)
            for b in range(ACT_ROWS):
                act.wait_ge(fin_ld[b], 16)
                for k in range(K):
                    ins = act.activation(weighed_sb[:, b, k, :], fin[:, b, k, :], ACT.Copy, scale=w_all[:, b, k:k + 1])
                ins.then_inc(weighed, 1)

        @block.tensor
        def _(pe):
            def busy(k):
                for _ in range(k):
                    pe.matmul(bank[7], ones_bf[:, :], ones_bf[:, None, :].to_broadcast([P, 4, P]), start=True, stop=True)

            pe.wait_ge(const_set, 1)
            busy(20)
            pe.wait_ge(cst_ld, 16)
            for b in range(B):
                if b % 4 == 0:
                    pe.wait_ge(y_done, b + 4)
                ins = pe.transpose(bank[b // 4][:, (b % 4) * P:(b % 4 + 1) * P], y_all[:, b, :], ident)
                if b % 4 == 3:
                    ins.then_inc(yT_mm, 1)

            def project(n, r, par):
                if isinstance(n, int):
                    yT, cT = yT_all[:, r, :], cT_all[:, r, :]
                else:
                    pe.wait_ge(yc_ld[par], 32 * n)
                    yT, cT = yc[:, par, 0, :], yc[:, par, 1, :]
                pe.matmul(bank[6][:, D:3 * D], ones_bf[0:3, :], small_rows[:, D:3 * D], start=True, stop=False)
                pe.matmul(bank[6][:, D:3 * D], cT, wkv_sb[:, :], start=False, stop=True)
                pe.matmul(bank[6][:, 0:D], ones_bf[0:3, :], small_rows[:, 0:D], start=True, stop=False)
                pe.matmul(bank[6][:, 0:D], yT, wq_sb[:, :], start=False, stop=True).then_inc(proj_mm, 1)

            def turn_parts(par_bank, which):
                for i in range(HP):
                    src = parts[:, which, 2 * i:2 * i + 2, :, :].rearrange("p h s d -> p (h s d)")
                    ins = pe.transpose(turned[par_bank][:, i * P:(i + 1) * P], src, id_bf[:, :])
                return ins

            def split_head(par, which, i, jj):
                return qk_sb[64 * jj:64 * jj + 64, par, which, i, :]

            def scores_half(half, par):
                for l in range(HP // 2):
                    for jj in range(2):
                        i = HP // 2 * half + l
                        ins = pe.matmul(scores[half][:, 512 * jj + P * l:512 * jj + P * l + P],
                                        split_head(par, 0, i, jj), split_head(par, 1, i, jj), start=True, stop=True)
                ins.then_inc(s_mm[half], 1)

            def shifted_half(half, par):
                for l in range(HP // 2):
                    for jj in range(2):
                        i = HP // 2 * half + l
                        dst = scores[half][:, 512 * jj + P * l:512 * jj + P * l + P]
                        pe.matmul(dst, sel[64 * jj:64 * jj + 64, i, :], mT_sb[64 * jj:64 * jj + 64, :],
                                  start=True, stop=False)
                        ins = pe.matmul(dst, split_head(par, 1, i, jj), split_head(par, 0, i, jj),
                                        start=False, stop=True)
                ins.then_inc(st_mm[half], 1)

            def weigh_values(half, par):
                for g in range(2 * half, 2 * half + 2):
                    for j in range(G):
                        h = G * g + j
                        ins = pe.matmul(bank[7][32 * j:32 * j + 32, g * P:(g + 1) * P], v_ext[:, par, h, :],
                                        pT[:, half, h % 2, h // 2 - HP // 2 * half, :], start=True, stop=True)
                return ins

            def step(n, par, a, b, c, p):
                t = 2 * n + par
                if b:
                    pe.wait_ge(mpart_done, t)
                    pe.transpose(m_turned, mx_part[:, :, :].rearrange("p j c -> p (j c)"), id_bf[:, :]).then_inc(m_turn_mm, 1)
                if a:
                    pe.wait_ge(kpart_done, t + 1)
                    if c:
                        pe.wait_ge(on_done, t - 1)
                    turn_parts(0, 1).then_inc(k_mm, 1)
                    pe.wait_ge(qpart_done, t + 1)
                    if c:
                        pe.wait_ge(x2_done, t - 1)
                    turn_parts(1, 0).then_inc(q_mm, 1)
                if c:
                    pe.wait_ge(tmp_done, t - 1)
                    if a:
                        pe.wait_ge(r1_done, t + 1)
                        pe.wait_ge(v_done, t + 1)
                    pe.transpose(bank[6][:, 0:P], tmp[:, :], ident).then_inc(tT_mm, 1)
                if not b and a:
                    busy(4)
                if b:
                    pe.wait_ge(mT_done, t)
                    shifted_half(0, 1 - par)
                if c:
                    pe.wait_ge(tT_done, t - 1)
                    if a:
                        pe.wait_ge(k_done, t + 1)
                    else:
                        pe.wait_ge(on_done, t - 1)
                    pe.matmul(g_ps, tT[:, :], gate_sb[:, :], start=True, stop=True).then_inc(gate_mm, 1)
                if b:
                    shifted_half(1, 1 - par)
                if a:
                    pe.wait_ge(k_done, t + 1)
                    pe.wait_ge(q_done, t + 1)
                if b:
                    pe.wait_ge(exp_done[0], t)
                if a:
                    scores_half(0, par)
                if b:
                    if c:
                        pe.wait_ge(oT_done, t - 1)
                    pe.wait_ge(v_done, t)
                    weigh_values(0, 1 - par)
                if c:
                    pe.wait_ge(m_done, t - 1)
                    pe.wait_ge(msum_done, t - 1)
                    pe.matmul(rank_ps, tri_bf[:, :], m_bf[:, :], start=True, stop=False)
                    pe.matmul(rank_ps, ones_bf[:, :], m_sum[:, :], start=False, stop=True).then_inc(rank_mm, 1)
                if b:
                    pe.wait_ge(exp_done[1], t)
                    weigh_values(1, 1 - par).then_inc(pv_mm, 1)
                if a:
                    scores_half(1, par)
                if p:
                    if not c:
                        pe.wait_ge(r1_done, t + 1)
                        pe.wait_ge(v_done, t + 1)
                    project(n, t + 1, 1 - par)
                if not b and a:
                    busy(8)
                if b:
                    pe.wait_ge(oT_done, t)
                    if c:
                        pe.wait_ge(place_done, t - 1)
                    for g in range(G):
                        ins = pe.transpose(bank[4][:, g * P:(g + 1) * P], oT[:, g, :], ident)
                    ins.then_inc(o_mm, 1)
                    busy(2)
                    pe.wait_ge(on_done, t)
                    pe.transpose(bank[5][:, 0:P], on[:, :], ident).then_inc(onT_mm, 1)
                    busy(2)
                    pe.wait_ge(onT_done, t)
                    pe.matmul(bank[5][:, P:P + D], onT[:, :], wo_sb[:, :], start=True, stop=True).then_inc(wo_mm, 1)
                    busy(2)

            pe.wait_ge(wqkv_ld, 32)
            pe.wait_ge(c_ld[0], 16)
            pe.wait_ge(sbias_out, 16)
            pe.wait_ge(yT_done, 1)
            project(0, 0, 0)
            pe.wait_ge(yT_done, 2)
            pe.wait_ge(c_ld[1], 16)
            pe.wait_ge(wo_ld, 32)
            busy(10)
            pe.wait_ge(const_set, 6)
            steps(step, pe)

            pe.wait_ge(msum_done, B + 1)
            pe.wait_ge(place_done, B)
            pe.matmul(bank[7][0:TILES, 0:E], ones_bf[:, 0:TILES], m_sum[:, :], start=True, stop=True).then_inc(cnt_mm, 1)
            pe.wait_ge(plan_step, 1)
            busy(9)
            pe.wait_ge(diag_done, 1)
            pe.matmul(bank[6][:, 0:4 * TILES], ones_f[0:TILES, :], diag[:, :, :], start=True, stop=True).then_inc(plan_mm, 1)

            def turn_rows(n, i):
                pe.wait_ge(xt_ld[i], 32 * n + 32)
                for h in range(2):
                    ins = pe.transpose(bank[4 + i % 2][:, h * P:(h + 1) * P], xt[:, i, h, 0:D], ident)
                ins.then_inc(xtT_mm, 1)

            ex = {}

            def pstep(n, i, xin, work, mid, end):
                q, par = U * n + i, i % 2
                def turn_next():
                    if from_slot(n, i, 1):
                        pe.wait_ge(xtT_done, q)
                    turn_rows(n if i < U - 1 else n + 1, (i + 1) % U)

                if xin and from_slot(n, i, 1):
                    turn_next()
                if i % 2 == 0:
                    if work:
                        ex["h"] = table(pe, mybir.EngineType.PE, 0, 2 * U * n + 2 * i, 4, E - 1)
                    if end:
                        ex["y"] = table(pe, mybir.EngineType.PE, 0, 2 * U * n + 2 * i - 6,
                                        2 if isinstance(n, int) and q == PAIRS + 2 else 4, E - 1)
                elif end and not from_slot(n, i, 4):
                    ex["y"] = [None, None] + table(pe, mybir.EngineType.PE, 0, 0, 2, E - 1)
                if mid:
                    pe.wait_ge(hid_done, q - 1)
                    if from_slot(n, i, 4):
                        pe.wait_ge(hidT_done, q - 3)
                    for h in range(2):
                        ins = pe.transpose(bank[6 + par][:, h * P:(h + 1) * P], hid[:, par, h, :], ident)
                    ins.then_inc(hidT_mm, 1)
                if end:
                    pe.wait_ge(hidT_done, q - 2)
                    for h in range(2):
                        e = ex["y"][2 * par + h]
                        dst = bank[3 - par][:, h * D:(h + 1) * D]
                        pe.matmul(dst, ones_bf[0:3, :], bias_rows[0:3, bass.ds(e * D + E * 2 * FF, D)],
                                  start=True, stop=False)
                        ins = pe.matmul(dst, hidT[:, 1 - par, h, :], w2_sb[:, bass.ds(e, 1), :],
                                        start=False, stop=True)
                    ins.then_inc(y_mm, 1)
                if work:
                    pe.wait_ge(xtT_done, q + 1)
                    if from_slot(n, i, 2):
                        pe.wait_ge(lin_done, q - 1)
                    for h in range(2):
                        e = ex["h"][2 * par + h]
                        dst = bank[par][:, h * 2 * FF:(h + 1) * 2 * FF]
                        pe.matmul(dst, ones_bf[0:3, :], bias_rows[0:3, bass.ds(e * (2 * FF), 2 * FF)],
                                  start=True, stop=False)
                        ins = pe.matmul(dst, xtT[:, par, h, :], w1_sb[:, bass.ds(e, 1), :],
                                        start=False, stop=True)
                    ins.then_inc(h_mm, 1)
                if not from_slot(n, i, 1):
                    turn_next()

            pe.wait_ge(ffw_ld, 16 * 2 * B)
            pe.wait_ge(bias_out, 48)
            busy(14)
            pe.wait_ge(inv_done, 1)
            turn_rows(0, 0)
            pair_steps(pstep, pe)

        @block.vector
        def _(dve):
            def split3(src, mid, dst, done):
                dve.tensor_copy(dst[:, 0, :], src).then_inc(done, 1)
                dve.wait_ge(done, 1)
                dve.tensor_tensor(mid[:, 0, :], src, dst[:, 0, :], ALU.subtract).then_inc(done, 1)
                dve.wait_ge(done, 2)
                dve.tensor_copy(dst[:, 1, :], mid[:, 0, :]).then_inc(done, 1)
                dve.wait_ge(done, 3)
                dve.tensor_tensor(mid[:, 1, :], mid[:, 0, :], dst[:, 1, :], ALU.subtract).then_inc(done, 1)
                dve.wait_ge(done, 4)
                dve.tensor_copy(dst[:, 2, :], mid[:, 1, :]).then_inc(done, 1)

            dve.memset(ones_bf[:, :], 1.0).then_inc(const_set, 1)
            dve.wait_ge(sbias_ld, 16)
            split3(sb_row[:, :], sb_res, sb_part, ssplit)
            for h in range(2):
                dve.wait_ge(x_ld[h], 16)
                for b in range(4 * h, 4 * h + 4):
                    dve.bn_stats(st1[:, b, :], x_sb[:, b, :]).then_inc(st1_done, 1)
                for b in range(4 * h, 4 * h + 4):
                    dve.wait_ge(st1_done, b + 1)
                    dve.bn_aggr(mv1[:, b, :], st1[:, b, :]).then_inc(mv1_done, 1)
                dve.wait_ge(mv1_done, 4 * h + 4)
                dve.tensor_scalar(ve1[:, 4 * h:4 * h + 4], mv1[:, 4 * h:4 * h + 4, 1], EPS, None,
                                  ALU.add).then_inc(ve1_done, 1)
            for b in range(B):
                dve.wait_ge(rs1_done, b // 4 + 1)
                dve.tensor_scalar(y_all[:, b, :], x_sb[:, b, :], mv1[:, b, 0:1], rs1[:, b:b + 1],
                                  ALU.subtract, ALU.mult).then_inc(y_done, 1)
            dve.wait_ge(cst_ld, 16)
            dve.tensor_copy(id_bf[:, :], ident).then_inc(const_set, 1)
            dve.tensor_copy(tri_bf[:, :], cst[:, C_TRI:C_TRI + P]).then_inc(const_set, 1)
            dve.tensor_scalar(sel[:, :, :], cst[:, C_IOTA:C_IOTA + HP, None].to_broadcast([P, HP, P]),
                              cst[:, C_PAIR:C_PAIR + 1], None, ALU.is_equal).then_inc(const_set, 1)
            dve.memset(ones_f[:, :], 1.0).then_inc(const_set, 1)
            dve.memset(ones_e[:, :], 1.0).then_inc(const_set, 1)
            dve.wait_ge(pool_set, 5)
            dve.wait_ge(xbo_done, 1)
            dve.wait_ge(ln_ld, 48)

            dve.wait_ge(bias_ld, 16)

            def second_part(which, slots):
                dve.tensor_copy(parts[:, which, :, slots, :],
                                res[:, which, :, None, :].to_broadcast([P, H, 3, DK])).then_inc(p2_done, 1)

            def third_part(which, second, slots, done):
                dve.tensor_tensor(parts[:, which, :, slots, :], res[:, which, :, None, :].to_broadcast([P, H, 2, DK]),
                                  parts[:, which, :, second, :], ALU.subtract).then_inc(done, 1)

            def row_max(half, jj):
                return dve.tensor_reduce(mx[:, jj, HP // 2 * half:HP // 2 * (half + 1)],
                                         scores[half][:, 512 * jj:512 * jj + 512].rearrange("p (i t) -> p i t", i=HP // 2),
                                         AX.X, ALU.max).then_inc(max_done, 1)

            def step(n, par, a, b, c, p):
                t = 2 * n + par
                if b:
                    dve.wait_ge(max_done, 4 * t)
                    dve.tensor_scalar(mx_part[:, :, 0:HP], mx[:, :, :], -1.0, None, ALU.mult).then_inc(neg_done, 1)
                if a:
                    dve.wait_ge(v_done, t + 1)
                    dve.tensor_tensor(res[:, :, :, :], bank[6][:, 0:2 * D].rearrange("p (i h d) -> p i h d", i=2, h=H),
                                      parts[:, :, :, 0, :], ALU.subtract).then_inc(r1_done, 1)
                if b:
                    dve.wait_ge(neg_done, t)
                    dve.scalar_tensor_tensor(out=mx_res[:, :, :], in0=mx[:, :, :], scalar=-1.0,
                                             in1=mx_part[:, :, 0:HP], op0=ALU.mult, op1=ALU.subtract).then_inc(mres_done, 1)
                if a:
                    dve.wait_ge(r1_done, t + 1)
                    second_part(1, slice(1, 8, 3))
                if b:
                    dve.wait_ge(mres_done, t)
                    dve.tensor_copy(mx_part[:, :, HP:2 * HP], mx_res[:, :, :]).then_inc(mhi_done, 1)
                if c:
                    dve.wait_ge(wo_mm, t - 1)
                    dve.tensor_tensor(x2[:, bass.ds(t - 2, 1), :], bank[5][:, P:P + D], xbo[:, bass.ds(t - 2, 1), :],
                                      ALU.add).then_inc(x2_done, 1)
                if b:
                    dve.wait_ge(mhi_done, t)
                    dve.tensor_tensor(mx_part[:, :, 2 * HP:3 * HP], mx_res[:, :, :], mx_part[:, :, HP:2 * HP],
                                      ALU.subtract).then_inc(mpart_done, 1)
                if a:
                    second_part(0, slice(3, 6))
                    dve.wait_ge(p2_done, 2 * t + 1)
                if c:
                    dve.wait_ge(x2_done, t - 1)
                if a:
                    third_part(1, slice(1, 5, 3), slice(2, 6, 3), kpart_done)
                if c:
                    dve.bn_stats(st2[:, :], x2[:, bass.ds(t - 2, 1), :]).then_inc(st2_done, 1)
                    dve.wait_ge(st2_done, t - 1)
                if a:
                    dve.wait_ge(p2_done, 2 * t + 2)
                    third_part(0, slice(3, 5), slice(6, 8), qpart_done)
                if c:
                    dve.bn_aggr(mv2[:, :], st2[:, :]).then_inc(mv2_done, 1)
                    dve.wait_ge(mv2_done, t - 1)
                    dve.tensor_scalar(ve2[:, :], mv2[:, 1:2], 1.0 + EPS, EPS * EPS, ALU.mult, ALU.add).then_inc(ve2_done, 1)
                    dve.scalar_tensor_tensor(out=tmp[:, :], in0=x2[:, bass.ds(t - 2, 1), :], scalar=mv2[:, 0:1],
                                             in1=sc_sb[:, :], op0=ALU.subtract, op1=ALU.mult).then_inc(tmp_done, 1)
                if a:
                    dve.wait_ge(q_mm, t + 1)
                    dve.tensor_copy(qk_sb[:, par, 0, :, :], turned[1].rearrange("p (i s) -> p i s", i=HP)).then_inc(q_done, 1)
                if not b and not c:
                    split3(b_sb[:, :], b_res, b_part, bsplit)
                if c:
                    dve.wait_ge(tmp_done, t - 1)
                    dve.wait_ge(rs2_done, t - 1)
                    dve.wait_ge(sent_rows[par], n)
                    dve.tensor_scalar(rows[:, par, :, 0:D], tmp[:, None, :].to_broadcast([P, K, D]), rs2[:, 0:1], None,
                                      ALU.mult).then_inc(t_done, 1)
                    dve.wait_ge(gate_mm, t - 1)
                    dve.scalar_tensor_tensor(out=g_sb[:, :], in0=g_ps, scalar=rs2[:, 0:1], in1=gb_sb[:, :],
                                             op0=ALU.mult, op1=ALU.add).then_inc(g_done, 1)
                    dve.wait_ge(g_done, t - 1)
                    dve.sem_inc(dve_turn, 1)
                    dve.max(top[:, :], g_sb[:, :]).then_inc(top_done, 1)
                    dve.wait_ge(top_done, t - 1)
                    dve.tensor_copy(top_all[:, bass.ds(t - 2, 1), :], top[:, 0:K]).then_inc(keep_done, 1)
                    dve.max_index(topi[:, :], top[:, :], g_sb[:, :]).then_inc(topi_done, 1)
                    dve.wait_ge(topi_done, t - 1)
                    dve.tensor_tensor(hot[:, :, :], cst[:, None, C_IOTA:C_IOTA + E].to_broadcast([P, K, E]),
                                      topi[:, 0:K, None].to_broadcast([P, K, E]), ALU.is_equal).then_inc(hot_done, 1)
                    dve.wait_ge(hot_done, t - 1)
                    dve.wait_ge(msum_done, t - 1)
                    with nc.allow_low_precision(reason="sums of at most four zeros and ones are exact"):
                        dve.tensor_reduce(m_bf[:, :], hot[:, :, :].rearrange("p k e -> p e k"), AX.X,
                                          ALU.add).then_inc(m_done, 1)
                if a:
                    dve.wait_ge(s_mm[0], t + 1)
                    if b:
                        dve.wait_ge(mres_done, t)
                    row_max(0, 0)
                    row_max(0, 1)
                if c:
                    dve.wait_ge(rank_mm, t - 1)
                    dve.tensor_tensor(place[:, :], rank_ps, cst[:, C_BASE:C_BASE + E], ALU.add).then_inc(place_done, 1)
                if a:
                    dve.wait_ge(s_mm[1], t + 1)
                    row_max(1, 0)
                if c:
                    dve.wait_ge(place_done, t - 1)
                    dve.tensor_tensor(pl_hot[:, :, :], hot[:, :, :], place[:, None, :].to_broadcast([P, K, E]),
                                      ALU.mult).then_inc(plhot_done, 1)
                if b:
                    o16 = bank[4].rearrange("p (h d) -> p h d", h=H)
                    dve.wait_ge(o_mm, t)
                    dve.reciprocal(rden[:, :, :], o16[:, :, DK:DK + 1]).then_inc(rden_done, 1)
                if c:
                    dve.wait_ge(plhot_done, t - 1)
                    with nc.allow_low_precision(reason="row numbers below 2**15 are exact"):
                        dve.tensor_reduce(pos[:, par, :], pl_hot[:, :, :], AX.X, ALU.add).then_inc(pos_done, 1)
                if b:
                    dve.wait_ge(rden_done, t)
                    dve.tensor_tensor(on[:, :].rearrange("p (h d) -> p h d", h=H), o16[:, :, 0:DK],
                                      rden[:, :, :].to_broadcast([P, H, DK]), ALU.mult).then_inc(on_done, 1)
                if a:
                    row_max(1, 1)

            steps(step, dve)
            dve.wait_ge(keep_done, B)
            dve.tensor_tensor(ew[:, :, :], top_all[:, :, :], top_all[:, :, 0:1].to_broadcast([P, B, K]),
                              ALU.subtract).then_inc(wsub_done, 1)

            dve.wait_ge(cnt_mm, 1)
            dve.tensor_copy(cnt[:, :], bank[7][0:TILES, 0:E]).then_inc(plan_step, 1)
            dve.wait_ge(plan_step, 1)
            dve.tensor_tensor(over[:, :, :], cnt[:, :, None].to_broadcast([TILES, E, B]),
                              cst[0:TILES, None, C_STEP:C_STEP + B].to_broadcast([TILES, E, B]),
                              ALU.is_gt).then_inc(plan_step, 1)
            dve.wait_ge(plan_step, 2)
            dve.tensor_reduce(nt[:, :], over[:, :, :], AX.X, ALU.add).then_inc(plan_step, 1)
            dve.wait_ge(plan_step, 3)
            dve.tensor_tensor_scan(incl[:, :], ones_e[:, :], nt[:, :], 0.0, ALU.mult, ALU.add).then_inc(plan_step, 1)
            dve.wait_ge(plan_step, 4)
            dve.tensor_tensor(excl[:, :], incl[:, :], nt[:, :], ALU.subtract).then_inc(plan_step, 1)
            dve.tensor_scalar(past[:, :], incl[:, :], cst[0:TILES, C_P:C_P + 1], None, ALU.is_le).then_inc(plan_step, 1)
            dve.wait_ge(plan_step, 6)
            dve.tensor_reduce(ecol[:, :], past[:, :], AX.X, ALU.add).then_inc(plan_step, 1)
            dve.wait_ge(plan_step, 7)
            dve.tensor_scalar(plan[:, 0:1], ecol[:, :], float(E - 1), None, ALU.min).then_inc(plan_step, 1)
            dve.wait_ge(plan_step, 8)
            dve.tensor_scalar(e_hot[:, :], cst[0:TILES, C_IOTA:C_IOTA + E], plan[:, 0:1], None,
                              ALU.is_equal).then_inc(plan_step, 1)
            dve.wait_ge(plan_step, 9)
            dve.tensor_tensor_reduce(out=junk[:, 0, :], in0=e_hot[:, :], in1=excl[:, :], scale=1.0, scalar=0.0,
                                     op0=ALU.mult, op1=ALU.add, accum_out=base_i[:, :]).then_inc(plan_step, 1)
            dve.tensor_tensor_reduce(out=junk[:, 1, :], in0=e_hot[:, :], in1=cnt[:, :], scale=1.0, scalar=0.0,
                                     op0=ALU.mult, op1=ALU.add, accum_out=cnt_i[:, :]).then_inc(plan_step, 1)
            dve.wait_ge(plan_step, 11)
            dve.tensor_scalar(a_i[:, :], base_i[:, :], cst[0:TILES, C_P:C_P + 1], -float(P), ALU.subtract,
                              ALU.mult).then_inc(plan_step, 1)
            dve.tensor_scalar(m_i[:, :], cnt_i[:, :], -float(P), 0.0, ALU.add, ALU.max).then_inc(plan_step, 1)
            dve.wait_ge(plan_step, 13)
            dve.tensor_tensor(r0_i[:, :], a_i[:, :], m_i[:, :], ALU.min).then_inc(plan_step, 1)
            dve.wait_ge(plan_step, 14)
            dve.scalar_tensor_tensor(out=plan[:, 1:2], in0=plan[:, 0:1], scalar=float(TOK), in1=r0_i[:, :],
                                     op0=ALU.mult, op1=ALU.add).then_inc(plan_step, 1)
            dve.tensor_tensor(plan[:, 2:3], a_i[:, :], r0_i[:, :], ALU.subtract).then_inc(plan_step, 1)
            dve.tensor_tensor(plan[:, 3:4], cnt_i[:, :], r0_i[:, :], ALU.subtract).then_inc(plan_step, 1)
            dve.wait_ge(plan_step, 17)
            dve.tensor_tensor(diag[:, :, :], cst[0:TILES, None, C_ID:C_ID + TILES].to_broadcast([TILES, 4, TILES]),
                              plan[:, :, None].to_broadcast([TILES, 4, TILES]), ALU.mult).then_inc(diag_done, 1)
            dve.wait_ge(plan_mm, 1)
            dve.tensor_copy(tab[:, :, :], bank[6][0:1, 0:2 * TILES].rearrange("p (a i) -> p a i", a=2)).then_inc(tab_done, 1)
            dve.tensor_scalar(inv[:, 0, :], bank[6][:, 2 * TILES:3 * TILES], cst[:, C_P:C_P + 1], None, ALU.is_gt)
            dve.tensor_scalar(inv[:, 1, :], bank[6][:, 3 * TILES:4 * TILES], cst[:, C_P:C_P + 1], None,
                              ALU.is_le).then_inc(inv_done, 1)
            dve.wait_ge(inv_done, 1)
            dve.tensor_tensor(inv[:, 2, :], inv[:, 0, :], inv[:, 1, :], ALU.max).then_inc(inv_done, 1)
            dve.wait_ge(inv_done, 2)
            dve.tensor_tensor(aside[:, :], inv[:, 2, :], cst[:, C_DUMMY:C_DUMMY + TILES], ALU.mult).then_inc(aside_done, 1)
            dve.wait_ge(aside_done, 1)

            def pstep(n, i, xin, work, mid, end):
                q, par = U * n + i, i % 2
                if end:
                    buf = (i + 1) % U
                    if from_slot(n, i, U + 3):
                        dve.wait_ge(back[buf], 32 * (n if i == U - 1 else n - 1))
                    dve.wait_ge(code_done, q - 2)
                    dve.sem_inc(dve_turn, 1)
                    dve.tensor_copy(dest[:, buf, :], dest_all[:, bass.ds(2 * U * n + 2 * i - 6, 2)]).then_inc(dest_done, 1)
                if work:
                    hb = bank[par][:, :].rearrange("p (i f) -> p i f", i=2)
                    dve.wait_ge(xt_ld[i], 32 * n + 32)
                    dve.tensor_tensor(dest_all[:, bass.ds(2 * U * n + 2 * i, 2)], xt[:, i, :, D],
                                      aside[:, bass.ds(2 * U * n + 2 * i, 2)], ALU.max).then_inc(code_done, 1)
                    dve.wait_ge(h_mm, q + 1)
                    dve.tensor_scalar(glu[:, par, :, :], hb[:, :, 0:FF], LIMIT, None, ALU.min).then_inc(glu_done, 1)
                    dve.tensor_scalar(lin[:, par, :, :], hb[:, :, FF:2 * FF], LIMIT, -LIMIT, ALU.min,
                                      ALU.max).then_inc(lin_done, 1)
                    dve.wait_ge(sg_done, q + 1)
                    dve.tensor_tensor(gs[:, par, :, :], glu[:, par, :, :], sg[:, par, :, :], ALU.mult).then_inc(gs_done, 1)
                    dve.wait_ge(gs_done, q + 1)
                    if from_slot(n, i, 2):
                        dve.wait_ge(hidT_mm, q - 1)
                    dve.scalar_tensor_tensor(out=hid[:, par, :, :], in0=lin[:, par, :, :], scalar=1.0,
                                             in1=gs[:, par, :, :], op0=ALU.add, op1=ALU.mult).then_inc(hid_done, 1)

            pair_steps(pstep, dve)

            for b in range(B):
                dve.bn_stats(st3[:, b, :], x2[:, b, :]).then_inc(st3_done, 1)
            for b in range(B):
                dve.wait_ge(st3_done, b + 1)
                dve.bn_aggr(mv3[:, b, :], st3[:, b, :]).then_inc(mv3_done, 1)
            dve.wait_ge(mv3_done, B)
            dve.tensor_scalar(ve3[:, :], mv3[:, :, 1], EPS, None, ALU.add).then_inc(ve3_done, 1)
            dve.wait_ge(ew_done, 1)
            dve.tensor_reduce(sw[:, :], ew[:, :, :], AX.X, ALU.add).then_inc(sw_done, 1)
            dve.wait_ge(sw_done, 1)
            dve.reciprocal(rsw[:, :], sw[:, :]).then_inc(rsw_done, 1)
            dve.wait_ge(rsw_done, 1)
            dve.tensor_tensor(w_all[:, :, :], ew[:, :, :], rsw[:, :, None].to_broadcast([P, B, K]),
                              ALU.mult).then_inc(w_done, 1)
            dve.wait_ge(rs3_done, 1)
            dve.tensor_scalar(a3[:, :], rs3[:, :], 1.0, None, ALU.add).then_inc(a3_done, 1)
            dve.tensor_tensor(c3[:, :], mv3[:, :, 0], rs3[:, :], ALU.mult).then_inc(a3_done, 1)
            dve.wait_ge(a3_done, 2)
            for b in range(B):
                dve.tensor_scalar(xr[:, b, :], x2[:, b, :], a3[:, b:b + 1], c3[:, b:b + 1],
                                  ALU.mult, ALU.subtract).then_inc(xr_done, 1)

            for bs in ([2, 3], [4, 5], [6, 7]):
                weighted_sum(dve, bs)


def kernel(x, ctx_1024, L0_xattn_wq, L0_xattn_bq, L0_xattn_wk, L0_xattn_bk, L0_xattn_wv, L0_xattn_bv,
           L0_xattn_wo, L0_xattn_bo, L0_ffn_norm_scale, L0_ffn_gate_w, L0_ffn_gate_b, L0_ffn_w1, L0_ffn_b1,
           L0_ffn_w2, L0_ffn_b2):
    import concourse.bacc as bacc
    from concourse.bass_utils import run_bass_kernel_spmd

    w1 = np.asarray(L0_ffn_w1).reshape(E, FF, 2, D)
    b1 = np.asarray(L0_ffn_b1).reshape(E, FF, 2).transpose(0, 2, 1).reshape(P, -1)
    b2 = np.asarray(L0_ffn_b2).reshape(P, -1)
    arrays = {
        "x": np.asarray(x).reshape(TOK, D),
        "ctxT": np.asarray(ctx_1024).reshape(TOK, D).T,
        "wqT": np.asarray(L0_xattn_wq).T,
        "wkvT": np.concatenate([np.asarray(L0_xattn_wk).T, np.asarray(L0_xattn_wv).T], axis=1),
        "small_b": np.concatenate([np.asarray(v) for v in (L0_xattn_bq, L0_xattn_bk, L0_xattn_bv)]).reshape(1, NB),
        "woT": np.asarray(L0_xattn_wo).T, "bo": np.asarray(L0_xattn_bo).reshape(1, D),
        "scale": np.asarray(L0_ffn_norm_scale).reshape(1, D),
        "gateT": np.asarray(L0_ffn_gate_w).T, "gate_b": np.asarray(L0_ffn_gate_b).reshape(1, E),
        "w1T": w1.transpose(3, 0, 2, 1).reshape(D, E, 2 * FF),
        "w2T": np.asarray(L0_ffn_w2).transpose(2, 0, 1),
        "b12": np.concatenate([b1, b2], axis=1),
        "consts": shape_constants(),
    }
    arrays = {k: np.ascontiguousarray(v) for k, v in arrays.items()}
    nc = bacc.Bacc("TRN2", target_bir_lowering=False, num_devices=1)
    args = {k: nc.dram_tensor(f"in_{k}", v.shape, mybir.dt.from_np(v.dtype), kind="ExternalInput").ap()
            for k, v in arrays.items()}
    out = nc.dram_tensor("out_0", (TOK, D), F32, kind="ExternalOutput").ap()
    build(nc, out=out, **args)
    r = run_bass_kernel_spmd(nc, [{f"in_{k}": v for k, v in arrays.items()}], core_ids=[0])
    return r.results[0]["out_0"].reshape(B, P, D)
```
